# Optimizing a Trainium2 kernel written in Bass

```python
import numpy as np
import jax
import jax.numpy as jnp

def _softmax(x, axis=-1):
    return jax.nn.softmax(x, axis=axis)
def _gelu(x):
    return jax.nn.gelu(x, approximate=True)
def _silu(x):
    return jax.nn.silu(x)
def _sigmoid(x):
    return jax.nn.sigmoid(x)
def _layernorm(x, axis=-1, eps=1e-5):
    m = jnp.mean(x, axis=axis, keepdims=True)
    v = jnp.var(x, axis=axis, keepdims=True)
    return (x - m) / jnp.sqrt(v + eps)
def _scatter_add(tgt, idx, src, axis=0):
    return tgt.at[idx].add(src)
def _segment_sum(src, seg, n):
    return jax.ops.segment_sum(src, seg, n)

kernel_name = 'mk_adj_resnorm_d2_adj_512_7d5a52'

def setup_inputs(seed: int = 0):
    np.random.seed(seed)
    _w = jnp.asarray
    def _rec_inputs():
        import jax
        import jax.numpy as jnp
        _gk = jax.random.key(seed)
        x = -0.0005207 + 1.001 * jax.random.normal(jax.random.fold_in(_gk, 1), (4096, 512), jnp.float32)
        _a = jax.random.bernoulli(jax.random.fold_in(_gk, 2), 0.00195312, (4096, 4096))
        _a = jnp.logical_or(_a, jnp.swapaxes(_a, -1, -2))
        _a = jnp.logical_or(_a, jnp.eye(4096, dtype=bool))
        adj = _a.astype(jnp.int32)
        return x, adj
    x, adj = _rec_inputs()
    def _L0_gnn_setup():
        import jax, jax.numpy as jnp
        import numpy as np
        N, NFEAT, NHEADS, C = (4096, 512, 8, 64)
        NEG_INF = -9000000000000000.0

        def glorot(key, shape):
            fan = shape[-2] + shape[-1]
            stdv = np.sqrt(6.0 / fan)
            return jax.random.uniform(key, shape, jnp.float32, -stdv, stdv)
        key = jax.random.key(seed)
        k_x, k_adj, k_w, k_al, k_ar = jax.random.split(key, 5)
        x = jax.random.normal(k_x, (N, NFEAT), jnp.float32)
        adj = jax.random.randint(k_adj, (N, N), 0, 2, jnp.int32)
        W = glorot(k_w, (NFEAT, NHEADS * C))
        b = jnp.zeros((NHEADS * C,), jnp.float32)
        att_l = glorot(k_al, (NHEADS, C))
        att_r = glorot(k_ar, (NHEADS, C))
        return {'x': x, 'adj': adj, 'W': W, 'b': b, 'att_l': att_l, 'att_r': att_r}
    _L0_gnn_all = _L0_gnn_setup()
    _L0_gnn_in = {k: v for k, v in _L0_gnn_all.items() if k in ('W', 'b', 'att_l', 'att_r', )}
    del _L0_gnn_all

    def _L1_gnn_setup():
        import jax, jax.numpy as jnp
        import numpy as np
        HEAD_SIZE = 8
        QK_DIM = 512
        V_DIM = 512
        N = 4096
        ATT_DIM = QK_DIM // HEAD_SIZE
        SCALE = ATT_DIM ** (-0.5)
        NEG_FILL = jnp.float32(-9000000000000000.0)
        key = jax.random.key(seed)
        k1, k2, k3, k4 = jax.random.split(key, 4)
        x1 = jax.random.normal(k1, (N, QK_DIM), dtype=jnp.float32)
        x2 = jax.random.normal(k2, (N, QK_DIM), dtype=jnp.float32)
        v = jax.random.normal(k3, (N, V_DIM), dtype=jnp.float32)
        adj = jax.random.randint(k4, (N, N), 0, 2, dtype=jnp.int32)
        return {'x1': x1, 'x2': x2, 'v': v, 'adj': adj}
    _L1_gnn_all = _L1_gnn_setup()
    _L1_gnn_in = {k: v for k, v in _L1_gnn_all.items() if k in ('x2', 'v', )}
    del _L1_gnn_all

    return {
        "x": x,
        "adj": adj,
        "L0_gnn_W": _L0_gnn_in["W"],
        "L0_gnn_b": _L0_gnn_in["b"],
        "L0_gnn_att_l": _L0_gnn_in["att_l"],
        "L0_gnn_att_r": _L0_gnn_in["att_r"],
        "L1_gnn_x2": _L1_gnn_in["x2"],
        "L1_gnn_v": _L1_gnn_in["v"],
    }

def reference(x, adj, L0_gnn_W, L0_gnn_b, L0_gnn_att_l, L0_gnn_att_r, L1_gnn_x2, L1_gnn_v):
    import jax
    import jax.numpy as jnp
    def _L0_gnn_ref(x, adj, W, b, att_l, att_r):
        import jax, jax.numpy as jnp
        import numpy as np
        N, NFEAT, NHEADS, C = (4096, 512, 8, 64)
        NEG_INF = -9000000000000000.0

        def glorot(key, shape):
            fan = shape[-2] + shape[-1]
            stdv = np.sqrt(6.0 / fan)
            return jax.random.uniform(key, shape, jnp.float32, -stdv, stdv)
        x_l = (x @ W + b).reshape(N, NHEADS, C)
        alpha_l = jnp.einsum('nhc,hc->nh', x_l, att_l)
        alpha_r = jnp.einsum('nhc,hc->nh', x_l, att_r)
        scores = alpha_l[:, None, :] * alpha_r[None, :, :]
        scores = jnp.where(adj[:, :, None] > 0, scores, NEG_INF)
        att = jax.nn.softmax(scores, axis=1)
        out = jnp.einsum('ijh,jhc->ihc', att, x_l)
        return jax.nn.relu(out.reshape(N, NHEADS * C))

    def _L1_gnn_ref(x1, x2, v, adj):
        import jax, jax.numpy as jnp
        import numpy as np
        HEAD_SIZE = 8
        QK_DIM = 512
        V_DIM = 512
        N = 4096
        ATT_DIM = QK_DIM // HEAD_SIZE
        SCALE = ATT_DIM ** (-0.5)
        NEG_FILL = jnp.float32(-9000000000000000.0)
        n = x1.shape[0]
        q = x1.reshape(n, HEAD_SIZE, -1).transpose(1, 0, 2) * SCALE
        k = x2.reshape(n, HEAD_SIZE, -1).transpose(1, 0, 2)
        vv = v.reshape(n, HEAD_SIZE, -1).transpose(1, 0, 2)
        scores = jnp.einsum('hnd,hmd->hnm', q, k)
        scores = jnp.where(adj > 0, scores, NEG_FILL)
        attn = jax.nn.softmax(scores, axis=-1)
        out = jnp.einsum('hnm,hmd->hnd', attn, vv)
        return out.transpose(1, 0, 2).reshape(n, -1)

    x = _layernorm(x + _L0_gnn_ref(x, adj, L0_gnn_W, L0_gnn_b, L0_gnn_att_l, L0_gnn_att_r), axis=-1)
    x = _layernorm(x + _L1_gnn_ref(x, L1_gnn_x2, L1_gnn_v, adj), axis=-1)
    return x


_drawn_inputs = setup_inputs


def setup_inputs(seed=0):
    import zlib

    import numpy as np

    out = dict(_drawn_inputs(seed))
    spreads = {'L0_gnn_b': (0.0, 0.1)}
    factors = {}
    for name, (base, spread) in spreads.items():
        noise = np.random.default_rng([zlib.crc32(name.encode()), seed]).standard_normal(out[name].shape)
        drawn = base * np.exp(spread * noise) if base else spread * noise
        out[name] = jnp.asarray(drawn.astype(out[name].dtype))
    for name, factor in factors.items():
        out[name] = (out[name] * factor).astype(out[name].dtype)
    return out
```

```python
from contextlib import ExitStack

import concourse.bass as bass
from concourse import mybir

F32 = mybir.dt.float32
F16 = mybir.dt.float16
BF16 = mybir.dt.bfloat16
I32 = mybir.dt.int32
U8 = mybir.dt.uint8
ALU = mybir.AluOpType
ACT = mybir.ActivationFunctionType
AX = mybir.AxisListType
ds = bass.ds

P = 128
N = 4096
F = 512
H = 8
C = F // H
NT = N // P
PAIRS = H // 2
IC = 1024
HALF = 512
CHUNKS = N // IC
JB = 8
KB = 4
NB = NT // JB
NP = 4
XW = 2 * C + 2
SCALE = float(C) ** -0.5
EPS = 1e-5


def gat_resnorm_kernel(nc, x, adj, W, b, att_l, att_r, x2, v, out):
    ctx = keep = ExitStack()
    with ctx:
        def sb(name, shape, dt, c=ctx):
            return c.enter_context(nc.sbuf_tensor(name, shape, dt))

        def ps(name, shape, dt, c):
            return c.enter_context(nc.psum_tensor(name, shape, dt))

        def sem(name, c=ctx):
            return c.enter_context(nc.semaphore(name))

        xl_dram = nc.dram_tensor("xl_scratch", [N, PAIRS, XW], F32).ap()
        al_dram = nc.dram_tensor("alpha_l_scratch", [H, N], F32).ap()
        k_dram = nc.dram_tensor("k_scratch", [2, F, N], F16).ap()
        q_dram = nc.dram_tensor("q_scratch", [2, F, N], F16).ap()
        shift_dram = nc.dram_tensor("shift_scratch", [2, H], F32).ap()
        o_dram = nc.dram_tensor("o_scratch", [2, PAIRS, P, N], F32).ap()
        d_dram = nc.dram_tensor("d_scratch", [2, H, N], F32).ap()
        x1_dram = nc.dram_tensor("x1_scratch", [N, F], F32).ap()

        maskT = sb("maskT", [P, NT, N], U8)
        identF = sb("identF", [P, P], F32)
        onesF = sb("onesF", [P, P], F32)
        colsum = sb("colsum", [H, 2, F], F32)
        kmax = sb("kmax", [H, 1], F32)

        prepare(nc, keep, x, adj, W, b, att_l, att_r, x2, v, xl_dram, al_dram, k_dram, shift_dram,
                maskT, identF, onesF, colsum, kmax)
        attend_gat(nc, keep, xl_dram, al_dram, shift_dram, o_dram, d_dram, maskT, onesF)
        finish_layer(nc, keep, 0, x, o_dram, d_dram, x1_dram, q_dram, shift_dram, identF, colsum, kmax)
        attend_dot(nc, keep, v, q_dram, k_dram, shift_dram, o_dram, d_dram, maskT, onesF)
        finish_layer(nc, keep, 1, x1_dram, o_dram, d_dram, out, None, None, identF, colsum, kmax)


def prepare(nc, keep, x, adj, W, b, att_l, att_r, x2, v, xl_dram, al_dram, k_dram, shift_dram,
            maskT, identF, onesF, colsum, kmax):
    ctx = ExitStack()
    with ctx:
        def sb(name, shape, dt):
            return ctx.enter_context(nc.sbuf_tensor(name, shape, dt))

        def ps(name, shape, dt):
            return ctx.enter_context(nc.psum_tensor(name, shape, dt))

        def sem(name):
            return keep.enter_context(nc.semaphore(name))

        QN = N // 4
        identB = sb("identB", [P, P], BF16)
        w_sb = sb("w_sb", [P, 4, F], F32)
        b_bc = sb("b_bc", [P, F], F32)
        att_bc = sb("att_bc", [P, 2, F], F32)
        wa_tmp = sb("wa_tmp", [P, F], F32)
        wa = sb("wa", [P, 4, 40], F32)
        ba = sb("ba", [P, 40], F32)
        headmask = sb("headmask", [H, F], F32)
        adj_sb = sb("adj_sb", [P, 2, QN], I32)
        mask_sb = sb("mask_sb", [P, 2, QN], BF16)
        x_sb = sb("x_sb", [P, 2, F], F32)
        x2_sb = sb("x2_sb", [P, 2, F], F32)
        v_sb = sb("v_sb", [P, 2, F], F32)
        xT = sb("xT", [P, 2, 4, P], F32)
        xl_sb = sb("xl_sb", [P, 2, PAIRS, XW], F32)
        kh = sb("kh", [P, PAIRS, KB * P], F16)
        kl = sb("kl", [P, PAIRS, KB * P], F16)
        sq = sb("sq", [P, F], F32)
        norms = sb("norms", [P, H], F32)
        norm_max = sb("norm_max", [P, H], F32)
        xl_sum = sb("xl_sum", [P, F], F32)
        v_sum = sb("v_sum", [P, F], F32)
        alphaT = sb("alphaT", [40, KB * P], F32)
        ext_new = sb("ext_new", [40, 2], F32)
        ext = sb("ext", [40, 4], F32)
        ext_r = sb("ext_r", [H, 2], F32)
        shift = sb("shift", [H, 1], F32)

        psX = ps("psX", [P, 4, P], F32)
        psK = ps("psK", [P, 4, P], F32)
        psL = ps("psL", [P, F], F32)
        psA = ps("psA", [P, 512], F32)
        psM = [ps(f"psM{i}", [P, JB, P], BF16) for i in range(4)]
        alpha_nat = psA[:, 0:H]
        alpha_T = psA[0:40, P:2 * P]

        zeroed = sem("zeroed")
        consts = sem("consts")
        w_loaded = sem("w_loaded")
        dve_step = sem("dve_step")
        wa_ready = sem("wa_ready")
        adj_loaded = [sem(f"adj_loaded{i}") for i in range(2)]
        x_loaded = [sem(f"x_loaded{i}") for i in range(2)]
        x2_loaded = [sem(f"x2_loaded{i}") for i in range(2)]
        v_loaded = [sem(f"v_loaded{i}") for i in range(2)]
        compared = [sem(f"compared{i}") for i in range(2)]
        turned = [sem(f"turned{i}") for i in range(4)]
        mask_out = [sem(f"mask_out{i}") for i in range(4)]
        x_turned = [sem(f"x_turned{i}") for i in range(2)]
        x2_turned = [sem(f"x2_turned{i}") for i in range(2)]
        xT_ready = [sem(f"xT_ready{i}") for i in range(2)]
        xl_ready = sem("xl_ready")
        alpha_ready = [sem(f"alpha_ready{i}") for i in range(2)]
        kh_ready = sem("kh_ready")
        kl_ready = sem("kl_ready")
        kl_round = sem("kl_round")
        squared = [sem(f"squared{i}") for i in range(2)]
        reduced = sem("reduced")
        normed = sem("normed")
        xl_done = [sem(f"xl_done{i}") for i in range(2)]
        alpha_done = sem("alpha_done")
        summed = [sem(f"summed{i}") for i in range(2)]
        v_summed = [sem(f"v_summed{i}") for i in range(2)]
        xl_stored = [sem(f"xl_stored{i}") for i in range(2)]
        k_stored = sem("k_stored")
        tail_pe = sem("tail_pe")
        tail_dve = sem("tail_dve")
        al_stored = sem("al_stored")
        ext_step = sem("ext_step")
        shift_stored = sem("shift_stored")

        block = ctx.enter_context(nc.Block())
        UN = KB
        R = NT // UN

        @block.sync
        def _(sp):
            sp.dma_start(w_sb[:], W.rearrange("(k p) n -> p k n", p=P)).then_inc(w_loaded, 16)
            sp.dma_start(b_bc[:], b.partition_broadcast(P)).then_inc(w_loaded, 16)
            sp.dma_start(att_bc[:, 0, :], att_l.rearrange("h c -> (h c)").partition_broadcast(P)).then_inc(w_loaded, 16)
            sp.dma_start(att_bc[:, 1, :], att_r.rearrange("h c -> (h c)").partition_broadcast(P)).then_inc(w_loaded, 16)
            with sp.Fori(0, R) as r:
                for s in range(UN):
                    k, t, m = s % 2, r * UN + s, r * (UN // 2) + s // 2
                    rows = ds(t * P, P)
                    sp.wait_ge(x_turned[k], m)
                    sp.dma_start(x_sb[:, k, :], x[rows, :]).then_inc(x_loaded[k], 16)
                    sp.wait_ge(x2_turned[k], m)
                    sp.wait_ge(squared[k], m)
                    sp.dma_start(x2_sb[:, k, :], x2[rows, :]).then_inc(x2_loaded[k], 16)
                    sp.wait_ge(v_summed[k], m)
                    sp.dma_start(v_sb[:, k, :], v[rows, :]).then_inc(v_loaded[k], 16)
                    for bank in range(4):
                        sp.wait_ge(compared[bank % 2], t * 2 + bank // 2)
                        sp.dma_start(adj_sb[:, bank % 2, :], adj[rows, bank * QN:(bank + 1) * QN]
                                     ).then_inc(adj_loaded[bank % 2], 16)

        @block.gpsimd
        def _(pool):
            pool.memset(identF[:], 0.0).then_inc(zeroed, 1)
            pool.memset(identB[:], 0.0).then_inc(zeroed, 1)
            pool.memset(headmask[:], 1.0).then_inc(zeroed, 1)
            pool.memset(onesF[:], 1.0).then_inc(consts, 1)
            pool.wait_ge(zeroed, 3)
            for ident in (identF, identB):
                pool.affine_select(out=ident[:], in_=ident[:], compare_op=ALU.not_equal, fill=1.0, base=0,
                                   pattern=[[-1, P]], channel_multiplier=1).then_inc(consts, 1)
            pool.affine_select(out=headmask[:], in_=headmask[:], compare_op=ALU.is_ge, fill=0.0, base=0,
                               pattern=[[1, F]], channel_multiplier=-C).then_inc(zeroed, 1)
            pool.wait_ge(zeroed, 4)
            pool.affine_select(out=headmask[:], in_=headmask[:], compare_op=ALU.is_ge, fill=0.0, base=C - 1,
                               pattern=[[-1, F]], channel_multiplier=C).then_inc(consts, 1)
            pool.memset(xl_sum[:], 0.0).then_inc(consts, 1)
            pool.memset(v_sum[:], 0.0).then_inc(consts, 1)
            pool.wait_ge(consts, 6)
            with pool.Fori(0, R) as r:
                for s in range(UN):
                    k, m = s % 2, r * (UN // 2) + s // 2
                    t = r * UN + s
                    pool.wait_ge(x2_loaded[k], m * 16 + 16)
                    pool.wait_ge(reduced, t)
                    pool.tensor_tensor(sq[:], x2_sb[:, k, :], x2_sb[:, k, :], ALU.mult).then_inc(squared[k], 1)
                    pool.wait_ge(v_loaded[k], m * 16 + 16)
                    if k == 1:
                        pool.wait_ge(v_summed[0], m + 1)
                    else:
                        pool.wait_ge(v_summed[1], m)
                    pool.tensor_tensor(v_sum[:], v_sum[:], v_sb[:, k, :], ALU.add).then_inc(v_summed[k], 1)
                    pool.wait_ge(xl_done[k], m * 2 + 2)
                    if k == 1:
                        pool.wait_ge(summed[0], m + 1)
                    else:
                        pool.wait_ge(summed[1], m)
                    pool.tensor_tensor(xl_sum[:].rearrange("p (a c) -> p a c", a=PAIRS),
                                       xl_sum[:].rearrange("p (a c) -> p a c", a=PAIRS),
                                       xl_sb[:, k, :, 0:2 * C], ALU.add).then_inc(summed[k], 1)
                    pool.dma_start(xl_dram[ds(t * P, P), :, :], xl_sb[:, k, :, :]).then_inc(xl_stored[k], 16)
                pool.wait_ge(kl_ready, r * UN + UN)
                for part, kk in enumerate((kh, kl)):
                    pool.dma_start(k_dram[part].rearrange("(a p) n -> p a n", p=P)[:, :, ds(r * (KB * P), KB * P)],
                                   kk[:]).then_inc(k_stored, 16)
                pool.wait_ge(alpha_done, r * UN + UN)
                pool.dma_start(al_dram[:, ds(r * (KB * P), KB * P)], alphaT[0:H, :]).then_inc(al_stored, 16)
            pool.wait_ge(tail_dve, 1)
            pool.dma_start(shift_dram[0].rearrange("(h o) -> h o", o=1), shift[:]).then_inc(shift_stored, 16)
            pool.wait_ge(shift_stored, 16)
            pool.wait_ge(al_stored, 16 * R)
            pool.wait_ge(k_stored, 32 * R)
            for k in range(2):
                pool.wait_ge(xl_stored[k], 16 * (NT // 2))

        @block.scalar
        def _(act):
            with act.Fori(0, R) as r:
                for s in range(UN):
                    k, t, m = s % 2, r * UN + s, r * (UN // 2) + s // 2
                    act.wait_ge(x_turned[k], m + 1)
                    act.wait_ge(alpha_ready[k], m)
                    nc.scalar.activation(xT[:, k, :, :], psX[:], ACT.Copy).then_inc(xT_ready[k], 1)
                    act.wait_ge(x2_turned[k], m + 1)
                    if s == 0:
                        act.wait_ge(k_stored, r * 32)
                    nc.scalar.activation(kh[:, :, s * P:(s + 1) * P], psK[:], ACT.Copy).then_inc(kh_ready, 1)
                    for bank in range(3):
                        act.wait_ge(turned[bank], t + 1)
                        nc.scalar.activation(maskT[:, bank * JB:(bank + 1) * JB, ds(t * P, P)], psM[bank][:],
                                             ACT.Copy).then_inc(mask_out[bank], 1)

        @block.tensor
        def _(pe):
            pe.wait_ge(consts, 6)
            pe.wait_ge(wa_ready, 1)
            with pe.Fori(0, R) as r:
                for s in range(UN):
                    k, t, m = s % 2, r * UN + s, r * (UN // 2) + s // 2
                    pe.wait_ge(x_loaded[k], m * 16 + 16)
                    if k == 1:
                        pe.wait_ge(xT_ready[0], m + 1)
                    else:
                        pe.wait_ge(xT_ready[1], m)
                    for c in range(4):
                        last = nc.tensor.transpose(psX[:, c, :], x_sb[:, k, c * P:(c + 1) * P], identF[:])
                    last.then_inc(x_turned[k], 1)
                    pe.wait_ge(x2_loaded[k], m * 16 + 16)
                    pe.wait_ge(kl_ready, t)
                    for c in range(4):
                        last = nc.tensor.transpose(psK[:, c, :], x2_sb[:, k, c * P:(c + 1) * P], identF[:])
                    last.then_inc(x2_turned[k], 1)
                    pe.wait_ge(xT_ready[k], m + 1)
                    if k == 1:
                        pe.wait_ge(xl_done[0], m * 2 + 2)
                    else:
                        pe.wait_ge(xl_done[1], m * 2)
                    for c in range(4):
                        last = nc.tensor.matmul(psL[:], xT[:, k, c, :], w_sb[:, c, :], start=(c == 0), stop=(c == 3))
                    last.then_inc(xl_ready, 1)
                    pe.wait_ge(alpha_done, t)
                    for c in range(4):
                        nc.tensor.matmul(alpha_nat, xT[:, k, c, :], wa[:, c, 32:40], start=(c == 0), stop=False)
                    nc.tensor.matmul(alpha_nat, onesF[0:1, :], ba[0:1, 32:40], start=False, stop=True)
                    for c in range(4):
                        nc.tensor.matmul(alpha_T, wa[:, c, :], xT[:, k, c, :], start=(c == 0), stop=False)
                    nc.tensor.matmul(alpha_T, ba[0:1, :], onesF[0:1, :], start=False,
                                     stop=True).then_inc(alpha_ready[k], 1)
                    for bank in range(4):
                        pe.wait_ge(compared[bank % 2], t * 2 + bank // 2 + 1)
                        pe.wait_ge(mask_out[bank], t)
                        for c in range(JB):
                            last = nc.tensor.transpose(psM[bank][:, c, :], mask_sb[:, bank % 2, c * P:(c + 1) * P],
                                                       identB[:])
                        last.then_inc(turned[bank], 1)
            for k in range(2):
                pe.wait_ge(summed[k], NT // 2)
                pe.wait_ge(v_summed[k], NT // 2)
            pe.wait_ge(kl_ready, NT)
            pe.wait_ge(xl_done[1], NT)
            nc.tensor.matmul(psL[0:H, :], onesF[:, 0:H], xl_sum[:], start=True, stop=True).then_inc(tail_pe, 1)
            nc.tensor.matmul(psK[0:H, :, :].rearrange("p a c -> p (a c)"), onesF[:, 0:H], v_sum[:],
                             start=True, stop=True).then_inc(tail_pe, 1)
            pe.wait_ge(normed, NT)
            nc.tensor.transpose(psX[0:H, 0, :], norm_max[:], identF[:]).then_inc(tail_pe, 1)

        @block.vector
        def _(dve):
            steps = [0]

            def then(ins):
                steps[0] += 1
                ins.then_inc(dve_step, 1)
                dve.wait_ge(dve_step, steps[0])

            nc.vector.memset(wa[:], 0.0)
            nc.vector.memset(norm_max[:], 0.0)
            then(nc.vector.memset(ba[:], 0.0))
            dve.wait_ge(w_loaded, 64)
            for a in range(2):
                for c in range(5):
                    src = w_sb[:, c, :] if c < 4 else b_bc[:]
                    dst = wa[:, c, 32 * a:32 * a + H] if c < 4 else ba[:, 32 * a:32 * a + H]
                    then(nc.vector.tensor_tensor(wa_tmp[:], src, att_bc[:, a, :], ALU.mult))
                    then(nc.vector.tensor_reduce(dst, wa_tmp[:].rearrange("p (h c) -> p h c", h=H), AX.X, ALU.add))
            nc.vector.memset(ext[:], 0.0).then_inc(wa_ready, 1)
            with dve.Fori(0, R) as r:
                for s in range(UN):
                    k, t, m = s % 2, r * UN + s, r * (UN // 2) + s // 2
                    for bank in range(4):
                        dve.wait_ge(adj_loaded[bank % 2], t * 32 + (bank // 2) * 16 + 16)
                        dve.wait_ge(turned[(bank + 2) % 4], t + (1 if bank >= 2 else 0))
                        nc.vector.tensor_scalar(mask_sb[:, bank % 2, :], adj_sb[:, bank % 2, :], 0.0, None,
                                                ALU.is_gt).then_inc(compared[bank % 2], 1)
                    dve.wait_ge(kh_ready, t + 1)
                    nc.vector.tensor_tensor(kl[:, :, s * P:(s + 1) * P], psK[:], kh[:, :, s * P:(s + 1) * P],
                                            ALU.subtract).then_inc(kl_ready, 1)
                    dve.wait_ge(squared[k], m + 1)
                    dve.wait_ge(normed, t)
                    nc.vector.tensor_reduce(norms[:], sq[:].rearrange("p (h c) -> p h c", h=H), AX.X,
                                            ALU.add).then_inc(reduced, 1)
                    dve.wait_ge(xl_ready, t + 1)
                    dve.wait_ge(xl_stored[k], m * 16)
                    dve.wait_ge(summed[k], m)
                    nc.vector.tensor_tensor(xl_sb[:, k, :, 0:2 * C], psL[:].rearrange("p (a c) -> p a c", a=PAIRS),
                                            b_bc[:].rearrange("p (a c) -> p a c", a=PAIRS),
                                            ALU.add).then_inc(xl_done[k], 1)
                    dve.wait_ge(reduced, t + 1)
                    nc.vector.tensor_tensor(norm_max[:], norm_max[:], norms[:], ALU.max).then_inc(normed, 1)
                    dve.wait_ge(alpha_ready[k], m + 1)
                    nc.vector.tensor_copy(xl_sb[:, k, :, 2 * C:XW],
                                          alpha_nat.rearrange("p (a h) -> p a h", h=2)).then_inc(xl_done[k], 1)
                    if s == 0:
                        dve.wait_ge(al_stored, r * 16)
                    nc.vector.tensor_copy(alphaT[:, s * P:(s + 1) * P], alpha_T).then_inc(alpha_done, 1)
                    dve.wait_ge(turned[3], t + 1)
                    nc.vector.tensor_copy(maskT[:, 3 * JB:4 * JB, ds(t * P, P)], psM[3][:]).then_inc(mask_out[3], 1)
                dve.wait_ge(alpha_done, r * UN + UN)
                for i, op in enumerate((ALU.max, ALU.min)):
                    nc.vector.tensor_reduce(ext_new[:, i:i + 1], alphaT[:], AX.X, op).then_inc(ext_step, 1)
                dve.wait_ge(ext_step, r * 4 + 2)
                for i, op in enumerate((ALU.max, ALU.min)):
                    nc.vector.tensor_tensor(ext[:, i:i + 1], ext[:, i:i + 1], ext_new[:, i:i + 1], op).then_inc(ext_step, 1)
                dve.wait_ge(ext_step, r * 4 + 4)
            then(nc.vector.tensor_scalar(ext[:, 2:3], ext[:, 1:2], -1.0, None, ALU.mult))
            then(nc.vector.tensor_tensor(ext[:, 3:4], ext[:, 0:1], ext[:, 2:3], ALU.max))
            then(nc.vector.tensor_copy(ext_r[:, 0:1], ext[32:40, 3:4]))
            then(nc.vector.tensor_tensor(ext_r[:, 1:2], ext[0:H, 3:4], ext_r[:, 0:1], ALU.mult))
            nc.vector.tensor_scalar(shift[:], ext_r[:, 1:2], -1.0, None, ALU.mult).then_inc(tail_dve, 1)
            dve.wait_ge(tail_pe, 1)
            nc.vector.tensor_tensor(colsum[:, 0, :], psL[0:H, :], headmask[:], ALU.mult)
            dve.wait_ge(tail_pe, 2)
            nc.vector.tensor_tensor(colsum[:, 1, :], psK[0:H, :, :].rearrange("p a c -> p (a c)"), headmask[:], ALU.mult)
            dve.wait_ge(tail_pe, 3)
            then(nc.vector.tensor_reduce(kmax[:], psX[0:H, 0, :], AX.X, ALU.max))


def attend_gat(nc, keep, xl_dram, al_dram, shift_dram, o_dram, d_dram, maskT, onesF):
    clear, accumulate = clear_with(nc), accumulate_with(nc)
    ctx = ExitStack()
    with ctx:
        def sb(name, shape, dt):
            return ctx.enter_context(nc.sbuf_tensor(name, shape, dt))

        def ps(name, shape, dt):
            return ctx.enter_context(nc.psum_tensor(name, shape, dt))

        def sem(name):
            return keep.enter_context(nc.semaphore(name))

        al_bc = sb("al_bc", [P, 2, 2, IC], F32)
        shift_bc = sb("g_shift", [P, 2, 2], F32)
        xl = sb("g_xl", [P, 2, KB, XW], F32)
        w = sb("g_weights", [P, NP, 2, IC], F32)
        o_sb = sb("g_o", [P, 2, IC], F32)
        d_sb = sb("g_d", [P, 2, HALF], F32)
        psO = [ps(f"g_psO{i}", [P, 2, HALF], F32) for i in range(2)]
        psD = [ps(f"g_psD{i}", [P, HALF], F32) for i in range(2)]
        zeros = sb("g_zeros", [1, HALF], BF16)
        zeros_set = sem("g_zeros_set")

        const_loaded = [sem(f"g_const_loaded{i}") for i in range(2)]
        const_used = [sem(f"g_const_used{i}") for i in range(2)]
        xl_loaded = [sem(f"g_xl_loaded{i}") for i in range(2)]
        exped = sem("g_exped")
        masked = sem("g_masked")
        w_used = [sem(f"g_w_used{u}") for u in range(JB)]
        evacuated = [sem(f"g_evacuated{i}") for i in range(2)]
        stored = [sem(f"g_stored{i}") for i in range(2)]

        block = ctx.enter_context(nc.Block())

        @block.sync
        def _(sp):
            with sp.Fori(0, CHUNKS) as ic:
                with sp.Fori(0, PAIRS // 2) as pp:
                    for par in range(2):
                        pair, use = pp * 2 + par, ic * (PAIRS // 2) + pp
                        sp.wait_ge(const_used[par], use)
                        sp.dma_start(al_bc[:, par, :, :],
                                     al_dram[ds(pair * 2, 2), ds(ic * IC, IC)].partition_broadcast(P)
                                     ).then_inc(const_loaded[par], 16)
                        sp.dma_start(shift_bc[:, par, :],
                                     shift_dram[0, ds(pair * 2, 2)].partition_broadcast(P)
                                     ).then_inc(const_loaded[par], 16)
                        with sp.Fori(0, NB) as q:
                            for slot in range(2):
                                B = (use * 2 + par) * NB + q
                                sp.wait_ge(w_used[slot * KB + KB - 1], B)
                                sp.dma_start(xl[:, slot, :, :],
                                             xl_dram[ds(q * (JB * P) + slot * (KB * P), KB * P), ds(pair, 1), :]
                                             .rearrange("(t p) a c -> p (t a) c", p=P)).then_inc(xl_loaded[slot], 16)

        @block.scalar
        def _(act):
            with act.Fori(0, CHUNKS * PAIRS // 2) as gg:
                for par in range(2):
                    act.wait_ge(const_loaded[par], gg * 32 + 32)
                    with act.Fori(0, NB) as q:
                        B = (gg * 2 + par) * NB + q
                        for u in range(JB):
                            slot = u // KB
                            if u % KB == 0:
                                act.wait_ge(xl_loaded[slot], B * 16 + 16)
                            wait_buffer(act, w_used, B, u)
                            for h in range(2):
                                last = nc.scalar.activation(w[:, u % NP, h, :], al_bc[:, par, h, :], ACT.Exp,
                                                            bias=shift_bc[:, par, h:h + 1],
                                                            scale=xl[:, slot, u % KB, 2 * C + h:2 * C + h + 1])
                                last.then_inc(exped, 1)
                    act.wait_ge(exped, (gg * 2 + par + 1) * (2 * NT))
                    act.sem_inc(const_used[par], 1)

        @block.vector
        def _(dve):
            with dve.Fori(0, CHUNKS) as ic:
                with dve.Fori(0, PAIRS // 2) as pp:
                    for par in range(2):
                        G = (ic * (PAIRS // 2) + pp) * 2 + par
                        with dve.Fori(0, NB) as q:
                            for u in range(JB):
                                n = (G * NB + q) * JB + u
                                for h in range(2):
                                    dve.wait_ge(exped, n * 2 + h + 1)
                                    nc.vector.tensor_tensor(w[:, u % NP, h, :], w[:, u % NP, h, :],
                                                            maskT[:, ds(q * JB + u, 1), ds(ic * IC, IC)]
                                                            .rearrange("p a c -> p (a c)"),
                                                            ALU.mult).then_inc(masked, 1)
                        dve.wait_ge(w_used[JB - 1], (G + 1) * NB)
                        use = ic * (PAIRS // 2) + pp
                        dve.wait_ge(stored[par], use * 48)
                        nc.vector.tensor_copy(o_sb[:, par, :], psO[par][:].rearrange("p a c -> p (a c)")).then_inc(evacuated[par], 1)
                        nc.vector.tensor_copy(d_sb[:, par, :], psD[par][:]).then_inc(evacuated[par], 1)

        @block.tensor
        def _(pe):
            pe.wait_ge(zeros_set, 1)
            with pe.Fori(0, CHUNKS * PAIRS // 2) as gg:
                for par in range(2):
                    pe.wait_ge(evacuated[par], gg * 2)
                    clear(psO[par], psD[par], zeros)
                    with pe.Fori(0, NB) as q:
                        B = (gg * 2 + par) * NB + q
                        for u in range(JB):
                            n, slot = B * JB + u, u // KB
                            pe.wait_ge(xl_loaded[slot], B * 16 + 16)
                            pe.wait_ge(masked, n * 2 + 2)
                            values = xl[:, slot, u % KB, 0:2 * C]
                            accumulate(w[:, u % NP, :, :], values, psO[par], psD[par], onesF
                                       ).then_inc(w_used[u], 1)

        @block.gpsimd
        def _(pool):
            pool.memset(zeros[:], 0.0).then_inc(zeros_set, 1)
            store_groups(pool, 0, o_sb, d_sb, evacuated, stored, o_dram, d_dram)


def clear_with(nc):
    def clear(psO, psD, zeros):
        for bank in (psO[:, 0, :], psO[:, 1, :], psD[:]):
            nc.tensor.matmul(bank, zeros[0:1, 0:P], zeros[0:1, :], start=True, stop=False, skip_group_check=True)
    return clear


def accumulate_with(nc):
    def accumulate(w, values, psO, psD, onesF):
        for hf in range(2):
            for h in range(2):
                nc.tensor.matmul(psO[h * C:(h + 1) * C, hf, :], values[:, h * C:(h + 1) * C],
                                 w[:, h, hf * HALF:(hf + 1) * HALF], start=False, stop=False, skip_group_check=True)
        for hf in range(2):
            for h in range(2):
                row = 32 * (2 * h + hf)
                last = nc.tensor.matmul(psD[row:row + 32, :], onesF[:, 0:32], w[:, h, hf * HALF:(hf + 1) * HALF],
                                        start=False, stop=False, skip_group_check=True)
        return last
    return accumulate


def wait_buffer(act, w_used, B, u):
    if u >= NP:
        act.wait_ge(w_used[u - NP], B + 1)
    else:
        act.wait_ge(w_used[u + JB - NP], B)


def store_groups(pool, layer, o_sb, d_sb, evacuated, stored, o_dram, d_dram):
    with pool.Fori(0, CHUNKS) as ic:
        with pool.Fori(0, PAIRS // 2) as pp:
            for par in range(2):
                pair, use = pp * 2 + par, ic * (PAIRS // 2) + pp
                pool.wait_ge(evacuated[par], use * 2 + 2)
                pool.dma_start(o_dram[layer, ds(pair, 1), :, ds(ic * IC, IC)].rearrange("a p n -> (a p) n"),
                               o_sb[:, par, :]).then_inc(stored[par], 16)
                for hf in range(2):
                    pool.dma_start(d_dram[layer, ds(pair * 2, 2), ds(ic * IC + hf * HALF, HALF)],
                                   d_sb[32 * hf:P:64, par, :]).then_inc(stored[par], 16)
    for par in range(2):
        pool.wait_ge(stored[par], 48 * CHUNKS * PAIRS // 2)


def finish_layer(nc, keep, layer, x, o_dram, d_dram, result, q_dram, shift_dram, identF, colsum, kmax):
    first = layer == 0
    ctx = ExitStack()
    with ctx:
        def sb(name, shape, dt):
            return ctx.enter_context(nc.sbuf_tensor(f"f{layer}_{name}", shape, dt))

        def ps(name, shape, dt):
            return ctx.enter_context(nc.psum_tensor(f"f{layer}_{name}", shape, dt))

        def sem(name):
            return keep.enter_context(nc.semaphore(f"f{layer}_{name}"))

        oT = sb("oT", [P, 2, PAIRS, P], F32)
        dT = sb("dT", [H, 2, P], F32)
        xin = sb("xin", [P, 2, F], F32)
        alone = sb("alone", [H, 2, P], F32)
        den = sb("den", [H, 2, P], F32)
        rden = sb("rden", [P, 2, H], F32)
        y = sb("y", [P, 2, F], F32)
        z = sb("z", [P, 2, F], F32)
        stats = sb("stats", [P, 2, 6], F32)
        mv = sb("mv", [P, 2, 2], F32)
        std = sb("std", [P, 2, 1], F32)
        rstd = sb("rstd", [P, 2, 1], F32)
        res = sb("res", [P, 2, F], F32)
        eps = sb("eps", [P, 1], F32)
        psO = [ps(f"psO{i}", [P, F], F32) for i in range(2)]
        psR = [ps(f"psR{i}", [P, H], F32) for i in range(2)]
        if first:
            qh = sb("qh", [P, PAIRS, KB * P], F16)
            ql = sb("ql", [P, PAIRS, KB * P], F16)
            sq = sb("sq", [P, 2, F], F32)
            norms = sb("norms", [P, H], F32)
            norm_max = sb("norm_max", [P, H], F32)
            qmax = sb("qmax", [H, 4], F32)
            psQ = [ps(f"psQ{i}", [P, 4, P], F32) for i in range(2)]

        eps_set = sem("eps_set")
        o_loaded = [sem(f"o_loaded{i}") for i in range(2)]
        d_loaded = [sem(f"d_loaded{i}") for i in range(2)]
        x_loaded = [sem(f"x_loaded{i}") for i in range(2)]
        den_ready = [sem(f"den_ready{i}") for i in range(2)]
        turned = [sem(f"turned{i}") for i in range(2)]
        chain = sem("chain")
        added = [sem(f"added{i}") for i in range(2)]
        stats_seen = sem("stats_seen")
        var_ready = sem("var_ready")
        std_ready = sem("std_ready")
        res_ready = [sem(f"res_ready{i}") for i in range(2)]
        res_stored = [sem(f"res_stored{i}") for i in range(2)]
        if first:
            q_turned = [sem(f"q_turned{i}") for i in range(2)]
            qh_ready = [sem(f"qh_ready{i}") for i in range(2)]
            ql_ready = [sem(f"ql_ready{i}") for i in range(2)]
            squared = [sem(f"squared{i}") for i in range(2)]
            reduced = [sem(f"reduced{i}") for i in range(2)]
            normed = sem("normed")
            q_stored = sem("q_stored")
            tail = sem("tail")
            s_stored = sem("s_stored")

        block = ctx.enter_context(nc.Block())
        UN = KB
        R = NT // UN

        @block.sync
        def _(sp):
            with sp.Fori(0, R) as r:
                for s in range(UN):
                    k, m, t = s % 2, r * (UN // 2) + s // 2, r * UN + s
                    sp.wait_ge(turned[k], m)
                    sp.dma_start(oT[:, k, :, :], o_dram[layer, :, :, ds(t * P, P)].rearrange("a p n -> p a n")
                                 ).then_inc(o_loaded[k], 16)
                    sp.wait_ge(den_ready[k], m)
                    sp.dma_start(dT[:, k, :], d_dram[layer, :, ds(t * P, P)]).then_inc(d_loaded[k], 16)
                    sp.wait_ge(added[k], m)
                    sp.dma_start(xin[:, k, :], x[ds(t * P, P), :]).then_inc(x_loaded[k], 16)

        @block.tensor
        def _(pe):
            with pe.Fori(0, R) as r:
                for s in range(UN):
                    k, m = s % 2, r * (UN // 2) + s // 2
                    pe.wait_ge(o_loaded[k], m * 16 + 16)
                    pe.wait_ge(den_ready[k], m + 1)
                    pe.wait_ge(added[k], m)
                    for a in range(PAIRS):
                        nc.tensor.matmul(psO[k][:, a * P:(a + 1) * P], oT[:, k, a, :], identF[:],
                                         start=(a == 0), stop=False, skip_group_check=True)
                    nc.tensor.matmul(psO[k][:], alone[:, k, :], colsum[:, layer, :], start=False, stop=True,
                                     skip_group_check=True)
                    nc.tensor.matmul(psR[k][:], den[:, k, :], identF[0:H, 0:H], start=True, stop=True
                                     ).then_inc(turned[k], 1)
                    if first:
                        pe.wait_ge(res_ready[k], m + 1)
                        pe.wait_ge(ql_ready[k], m)
                        for a in range(4):
                            last = nc.tensor.transpose(psQ[k][:, a, :], res[:, k, a * P:(a + 1) * P], identF[:])
                        last.then_inc(q_turned[k], 1)
            if first:
                pe.wait_ge(normed, NT)
                pe.wait_ge(added[0], NT // 2)
                nc.tensor.transpose(psO[0][0:H, 0:P], norm_max[:], identF[:]).then_inc(tail, 1)

        @block.scalar
        def _(act):
            with act.Fori(0, R) as r:
                for s in range(UN):
                    k, m, t = s % 2, r * (UN // 2) + s // 2, r * UN + s
                    act.wait_ge(eps_set, 1)
                    act.wait_ge(var_ready, t + 1)
                    nc.scalar.activation(std[:, k, :], mv[:, k, 1:2], ACT.Sqrt, bias=eps[:]).then_inc(std_ready, 1)
                    act.wait_ge(res_ready[k], m + 1)
                    act.dma_start(result[ds(t * P, P), :], res[:, k, :]).then_inc(res_stored[k], 16)
                    if first:
                        act.wait_ge(q_turned[k], m + 1)
                        if s == 0:
                            act.wait_ge(q_stored, r * 32)
                        nc.scalar.activation(qh[:, :, s * P:(s + 1) * P], psQ[k][:], ACT.Copy).then_inc(qh_ready[k], 1)
            if first:
                act.wait_ge(tail, 3)
                nc.scalar.activation(qmax[:, 2:3], qmax[:, 1:2], ACT.Sqrt).then_inc(tail, 1)
            for k in range(2):
                act.wait_ge(res_stored[k], 16 * NT // 2)

        @block.gpsimd
        def _(pool):
            if first:
                with pool.Fori(0, R) as r:
                    for s in range(UN):
                        k, m = s % 2, r * (UN // 2) + s // 2
                        pool.wait_ge(res_ready[k], m + 1)
                        pool.wait_ge(reduced[k], m)
                        pool.tensor_tensor(sq[:, k, :], res[:, k, :], res[:, k, :], ALU.mult).then_inc(squared[k], 1)
                    for k in range(2):
                        pool.wait_ge(ql_ready[k], r * (UN // 2) + UN // 2)
                    for part, qq in enumerate((qh, ql)):
                        pool.dma_start(q_dram[part].rearrange("(a p) n -> p a n", p=P)[:, :, ds(r * (KB * P), KB * P)],
                                       qq[:]).then_inc(q_stored, 16)
                pool.wait_ge(tail, 5)
                pool.dma_start(shift_dram[1].rearrange("(h o) -> h o", o=1), qmax[:, 3:4]).then_inc(s_stored, 16)
                pool.wait_ge(s_stored, 16)
                pool.wait_ge(q_stored, 32 * R)

        @block.vector
        def _(dve):
            nc.vector.memset(eps[:], EPS).then_inc(eps_set, 1)
            if first:
                nc.vector.memset(norm_max[:], 0.0)
            LINKS = 6 if first else 5
            with dve.Fori(0, R) as r:
                for s in range(UN):
                    k, m, t = s % 2, r * (UN // 2) + s // 2, r * UN + s
                    link = [0]

                    def then(ins):
                        link[0] += 1
                        ins.then_inc(chain, 1)
                        dve.wait_ge(chain, t * LINKS + link[0])

                    dve.wait_ge(d_loaded[k], m * 16 + 16)
                    dve.wait_ge(turned[k], m)
                    then(nc.vector.tensor_scalar(alone[:, k, :], dT[:, k, :], 0.0, None, ALU.is_equal))
                    nc.vector.scalar_tensor_tensor(out=den[:, k, :], in0=alone[:, k, :], scalar=float(N),
                                                   in1=dT[:, k, :], op0=ALU.mult, op1=ALU.add).then_inc(den_ready[k], 1)
                    dve.wait_ge(turned[k], m + 1)
                    then(nc.vector.reciprocal(rden[:, k, :], psR[k][:]))
                    then(nc.vector.tensor_tensor(y[:, k, :].rearrange("p (h c) -> p h c", h=H),
                                                 psO[k][:].rearrange("p (h c) -> p h c", h=H),
                                                 rden[:, k, :].unsqueeze(2).to_broadcast([P, H, C]), ALU.mult))
                    dve.wait_ge(x_loaded[k], m * 16 + 16)
                    if first:
                        ins = nc.vector.scalar_tensor_tensor(out=z[:, k, :], in0=y[:, k, :], scalar=0.0,
                                                             in1=xin[:, k, :], op0=ALU.max, op1=ALU.add)
                    else:
                        ins = nc.vector.tensor_tensor(z[:, k, :], y[:, k, :], xin[:, k, :], ALU.add)
                    ins.then_inc(added[k], 1)
                    dve.wait_ge(added[k], m + 1)
                    nc.vector.bn_stats(stats[:, k, :], z[:, k, :]).then_inc(chain, 1)
                    link[0] += 1
                    dve.wait_ge(chain, t * LINKS + link[0])
                    dve.sem_inc(stats_seen, 1)
                    nc.vector.bn_aggr(mv[:, k, :], stats[:, k, :]).then_inc(var_ready, 1)
                    dve.wait_ge(std_ready, t + 1)
                    then(nc.vector.reciprocal(rstd[:, k, :], std[:, k, :]))
                    dve.wait_ge(res_stored[k], m * 16)
                    if first:
                        dve.wait_ge(q_turned[k], m)
                        dve.wait_ge(squared[k], m)
                    nc.vector.tensor_scalar(res[:, k, :], z[:, k, :], mv[:, k, 0:1], rstd[:, k, 0:1],
                                            ALU.subtract, ALU.mult).then_inc(res_ready[k], 1)
                    if first:
                        dve.wait_ge(squared[k], m + 1)
                        then(nc.vector.tensor_reduce(norms[:], sq[:, k, :].rearrange("p (h c) -> p h c", h=H), AX.X, ALU.add))
                        nc.vector.tensor_tensor(norm_max[:], norm_max[:], norms[:], ALU.max).then_inc(normed, 1)
                        nc.vector.sem_inc(reduced[k], 1)
                        dve.wait_ge(qh_ready[k], m + 1)
                        nc.vector.tensor_tensor(ql[:, :, s * P:(s + 1) * P], psQ[k][:], qh[:, :, s * P:(s + 1) * P],
                                                ALU.subtract).then_inc(ql_ready[k], 1)
            if first:
                dve.wait_ge(tail, 1)
                nc.vector.tensor_reduce(qmax[:, 0:1], psO[0][0:H, 0:P], AX.X, ALU.max).then_inc(tail, 1)
                dve.wait_ge(tail, 2)
                nc.vector.tensor_tensor(qmax[:, 1:2], qmax[:, 0:1], kmax[:], ALU.mult).then_inc(tail, 1)
                dve.wait_ge(tail, 4)
                nc.vector.tensor_scalar(qmax[:, 3:4], qmax[:, 2:3], -SCALE, None, ALU.mult).then_inc(tail, 1)


def attend_dot(nc, keep, v, q_dram, k_dram, shift_dram, o_dram, d_dram, maskT, onesF):
    clear, accumulate = clear_with(nc), accumulate_with(nc)
    ctx = ExitStack()
    with ctx:
        def sb(name, shape, dt):
            return ctx.enter_context(nc.sbuf_tensor(f"a_{name}", shape, dt))

        def ps(name, shape, dt):
            return ctx.enter_context(nc.psum_tensor(f"a_{name}", shape, dt))

        def sem(name):
            return keep.enter_context(nc.semaphore(f"a_{name}"))

        q_sb = sb("q", [P, 2, 2, 2, IC], F16)
        shift_bc = sb("shift", [P, 2, 2], F32)
        k_sb = sb("k", [P, 2, 2, KB * P], F16)
        v_sb = sb("v", [P, 2, KB, 2 * C], F32)
        w = sb("weights", [P, NP, 2, IC], F32)
        o_sb = sb("o", [P, 2, IC], F32)
        d_sb = sb("d", [P, 2, HALF], F32)
        zeros = sb("zeros", [1, HALF], BF16)
        psS = [ps(f"psS{i}", [P, 2, HALF], F32) for i in range(2)]
        psO = ps("psO", [P, 2, HALF], F32)
        psD = ps("psD", [P, HALF], F32)

        zeros_set = sem("zeros_set")
        q_loaded = [sem(f"q_loaded{i}") for i in range(2)]
        k_loaded = [sem(f"k_loaded{i}") for i in range(2)]
        v_loaded = [sem(f"v_loaded{i}") for i in range(2)]
        scored = [[sem(f"scored{h}_{slot}") for slot in range(2)] for h in range(2)]
        exped = [sem(f"exped{i}") for i in range(2)]
        masked = sem("masked")
        w_used = [sem(f"w_used{u}") for u in range(JB)]
        evacuated = [sem(f"evacuated{i}") for i in range(2)]
        stored = [sem(f"stored{i}") for i in range(2)]

        block = ctx.enter_context(nc.Block())
        GG = CHUNKS * PAIRS // 2

        @block.sync
        def _(sp):
            with sp.Fori(0, CHUNKS) as ic:
                with sp.Fori(0, PAIRS // 2) as pp:
                    for par in range(2):
                        pair, use = pp * 2 + par, ic * (PAIRS // 2) + pp
                        G = use * 2 + par
                        sp.wait_ge(evacuated[par], use * 2)
                        for twice in range(2):
                            for part in range(2):
                                sp.dma_start(q_sb[twice * C:(twice + 1) * C, par, part, :, :],
                                             q_dram[part, ds(pair * (2 * C), 2 * C), ds(ic * IC, IC)]
                                             .rearrange("(h c) n -> c h n", h=2)).then_inc(q_loaded[par], 16)
                        sp.dma_start(shift_bc[:, par, :], shift_dram[1, ds(pair * 2, 2)].partition_broadcast(P)
                                     ).then_inc(q_loaded[par], 16)
                        with sp.Fori(0, NB) as q:
                            for slot in range(2):
                                B = G * NB + q
                                src = q * (JB * P) + slot * (KB * P)
                                sp.wait_ge(scored[1][slot], B * KB)
                                for part in range(2):
                                    sp.dma_start(k_sb[part * C:(part + 1) * C, slot, :, :],
                                                 k_dram[part, ds(pair * (2 * C), 2 * C), ds(src, KB * P)]
                                                 .rearrange("(h c) n -> c h n", h=2)).then_inc(k_loaded[slot], 16)
                                sp.wait_ge(w_used[slot * KB + KB - 1], B)
                                sp.dma_start(v_sb[:, slot, :, :],
                                             v[ds(src, KB * P), ds(pair * (2 * C), 2 * C)]
                                             .rearrange("(t p) c -> p t c", p=P)).then_inc(v_loaded[slot], 16)

        @block.tensor
        def _(pe):
            def scores(B, u, par):
                n, slot = B * JB + u, u // KB
                if u % KB == 0:
                    pe.wait_ge(k_loaded[slot], B * 32 + 32)
                for h in range(2):
                    pe.wait_ge(exped[h], n)
                    for hf in range(2):
                        for part in range(2):
                            last = nc.tensor.matmul(psS[h][:, hf, :],
                                                    k_sb[:, slot, h, (u % KB) * P:(u % KB + 1) * P],
                                                    q_sb[:, par, part, h, hf * HALF:(hf + 1) * HALF],
                                                    start=(part == 0), stop=(part == 1))
                    last.then_inc(scored[h][slot], 1)

            def sums(B, u):
                n, slot = B * JB + u, u // KB
                if u % KB == 0:
                    pe.wait_ge(v_loaded[slot], B * 16 + 16)
                pe.wait_ge(masked, n * 2 + 2)
                accumulate(w[:, u % NP, :, :], v_sb[:, slot, u % KB, :], psO, psD, onesF).then_inc(w_used[u], 1)

            pe.wait_ge(zeros_set, 1)
            with pe.Fori(0, GG) as gg:
                for par in range(2):
                    G = gg * 2 + par
                    if par == 0:
                        pe.wait_ge(q_loaded[0], gg * 80 + 80)
                        scores(G * NB, 0, 0)
                    pe.wait_ge(evacuated[1 - par], gg * 2 + 2 * par)
                    clear(psO, psD, zeros)
                    with pe.Fori(0, NB - 1) as q:
                        for u in range(JB):
                            B = G * NB + q
                            scores(B + (u + 1) // JB, (u + 1) % JB, par)
                            sums(B, u)
                    B = G * NB + (NB - 1)
                    for u in range(JB):
                        if u < JB - 1:
                            scores(B, u + 1, par)
                        elif par == 0:
                            pe.wait_ge(q_loaded[1], gg * 80 + 80)
                            scores(B + 1, 0, 1)
                        sums(B, u)

        @block.scalar
        def _(act):
            with act.Fori(0, GG) as gg:
                for par in range(2):
                    act.wait_ge(q_loaded[par], gg * 80 + 80)
                    with act.Fori(0, NB) as q:
                        B = (gg * 2 + par) * NB + q
                        for u in range(JB):
                            wait_buffer(act, w_used, B, u)
                            for h in range(2):
                                act.wait_ge(scored[h][u // KB], B * KB + u % KB + 1)
                                nc.scalar.activation(w[:, u % NP, h, :], psS[h][:].rearrange("p a c -> p (a c)"), ACT.Exp,
                                                     bias=shift_bc[:, par, h:h + 1], scale=SCALE).then_inc(exped[h], 1)

        @block.vector
        def _(dve):
            with dve.Fori(0, CHUNKS) as ic:
                with dve.Fori(0, PAIRS // 2) as pp:
                    for par in range(2):
                        use = ic * (PAIRS // 2) + pp
                        G = use * 2 + par
                        with dve.Fori(0, NB) as q:
                            for u in range(JB):
                                n = (G * NB + q) * JB + u
                                for h in range(2):
                                    dve.wait_ge(exped[h], n + 1)
                                    nc.vector.tensor_tensor(w[:, u % NP, h, :], w[:, u % NP, h, :],
                                                            maskT[:, ds(q * JB + u, 1), ds(ic * IC, IC)]
                                                            .rearrange("p a c -> p (a c)"),
                                                            ALU.mult).then_inc(masked, 1)
                        dve.wait_ge(w_used[JB - 1], (G + 1) * NB)
                        dve.wait_ge(stored[par], use * 48)
                        nc.vector.tensor_copy(o_sb[:, par, :], psO[:].rearrange("p a c -> p (a c)")).then_inc(evacuated[par], 1)
                        nc.vector.tensor_copy(d_sb[:, par, :], psD[:]).then_inc(evacuated[par], 1)

        @block.gpsimd
        def _(pool):
            pool.memset(zeros[:], 0.0).then_inc(zeros_set, 1)
            store_groups(pool, 1, o_sb, d_sb, evacuated, stored, o_dram, d_dram)


_INS = ["x", "adj", "L0_gnn_W", "L0_gnn_b", "L0_gnn_att_l", "L0_gnn_att_r", "L1_gnn_x2", "L1_gnn_v"]


def kernel(**inputs):
    import numpy as _np
    import concourse.bacc as _bacc
    from concourse import mybir as _mybir
    from concourse.bass_utils import run_bass_kernel_spmd as _run

    nc = _bacc.Bacc("TRN2", target_bir_lowering=False, num_devices=1)
    arrays, args = {}, []
    for name in _INS:
        a = _np.ascontiguousarray(inputs[name])
        arrays[f"in_{name}_dram"] = a
        args.append(nc.dram_tensor(f"in_{name}_dram", a.shape, _mybir.dt.from_np(a.dtype), kind="ExternalInput").ap())
    args.append(nc.dram_tensor("out_0_dram", (N, F), F32, kind="ExternalOutput").ap())
    gat_resnorm_kernel(nc, *args)
    r = _run(nc, [arrays], core_ids=[0])
    return r.results[0]["out_0_dram"]
```

```python
from contextlib import ExitStack

import concourse.bass as bass
from concourse import mybir

F32 = mybir.dt.float32
F16 = mybir.dt.float16
BF16 = mybir.dt.bfloat16
I32 = mybir.dt.int32
U8 = mybir.dt.uint8
ALU = mybir.AluOpType
ACT = mybir.ActivationFunctionType
AX = mybir.AxisListType
ds = bass.ds

P = 128
N = 4096
F = 512
H = 8
C = F // H
NT = N // P
PAIRS = H // 2
IC = 1024
HALF = 512
CHUNKS = N // IC
JB = 8
KB = 4
NB = NT // JB
NP = 4
SETS = ((0, 1, 2), (3, 4, 5), (6, 7))
XW = 2 * C + 2
SCALE = float(C) ** -0.5
EPS = 1e-5


def gat_resnorm_kernel(nc, x, adj, W, b, att_l, att_r, x2, v, out):
    ctx = keep = ExitStack()
    with ctx:
        def sb(name, shape, dt, c=ctx):
            return c.enter_context(nc.sbuf_tensor(name, shape, dt))

        def ps(name, shape, dt, c):
            return c.enter_context(nc.psum_tensor(name, shape, dt))

        def sem(name, c=ctx):
            return c.enter_context(nc.semaphore(name))

        xl_dram = nc.dram_tensor("xl_scratch", [N, PAIRS, XW], F32).ap()
        al_dram = nc.dram_tensor("alpha_l_scratch", [H, N], F32).ap()
        k_dram = nc.dram_tensor("k_scratch", [2, F, N], F16).ap()
        q_dram = nc.dram_tensor("q_scratch", [2, F, N], F16).ap()
        shift_dram = nc.dram_tensor("shift_scratch", [2, H], F32).ap()
        o_dram = nc.dram_tensor("o_scratch", [2, PAIRS, P, N], F32).ap()
        d_dram = nc.dram_tensor("d_scratch", [2, H, N], F32).ap()
        x1_dram = nc.dram_tensor("x1_scratch", [N, F], F32).ap()

        maskT = sb("maskT", [P, NT, N], U8)
        identF = sb("identF", [P, P], F32)
        onesF = sb("onesF", [P, P], F32)
        colsum = sb("colsum", [H, 2, F], F32)
        kmax = sb("kmax", [H, 1], F32)

        prepare(nc, keep, x, adj, W, b, att_l, att_r, x2, v, xl_dram, al_dram, k_dram, shift_dram,
                maskT, identF, onesF, colsum, kmax)
        attend_gat(nc, keep, xl_dram, al_dram, shift_dram, o_dram, d_dram, maskT, onesF)
        finish_layer(nc, keep, 0, x, o_dram, d_dram, x1_dram, q_dram, shift_dram, identF, colsum, kmax)
        attend_dot(nc, keep, v, q_dram, k_dram, shift_dram, o_dram, d_dram, maskT, onesF)
        finish_layer(nc, keep, 1, x1_dram, o_dram, d_dram, out, None, None, identF, colsum, kmax)


def prepare(nc, keep, x, adj, W, b, att_l, att_r, x2, v, xl_dram, al_dram, k_dram, shift_dram,
            maskT, identF, onesF, colsum, kmax):
    ctx = ExitStack()
    with ctx:
        def sb(name, shape, dt):
            return ctx.enter_context(nc.sbuf_tensor(name, shape, dt))

        def ps(name, shape, dt):
            return ctx.enter_context(nc.psum_tensor(name, shape, dt))

        def sem(name):
            return keep.enter_context(nc.semaphore(name))

        QN = N // 4
        identB = sb("identB", [P, P], BF16)
        w_sb = sb("w_sb", [P, 4, F], F32)
        b_bc = sb("b_bc", [P, F], F32)
        att_bc = sb("att_bc", [P, 2, F], F32)
        wa_tmp = sb("wa_tmp", [P, F], F32)
        wa = sb("wa", [P, 4, 40], F32)
        ba = sb("ba", [P, 40], F32)
        headmask = sb("headmask", [H, F], F32)
        adj_sb = sb("adj_sb", [P, 2, QN], I32)
        mask_sb = sb("mask_sb", [P, 2, QN], BF16)
        x_sb = sb("x_sb", [P, 2, F], F32)
        x2_sb = sb("x2_sb", [P, 2, F], F32)
        v_sb = sb("v_sb", [P, 2, F], F32)
        xT = sb("xT", [P, 2, 4, P], F32)
        xl_sb = sb("xl_sb", [P, 2, PAIRS, XW], F32)
        kh = sb("kh", [P, PAIRS, KB * P], F16)
        kl = sb("kl", [P, PAIRS, KB * P], F16)
        sq = sb("sq", [P, F], F32)
        norms = sb("norms", [P, H], F32)
        norm_max = sb("norm_max", [P, H], F32)
        xl_sum = sb("xl_sum", [P, F], F32)
        v_sum = sb("v_sum", [P, F], F32)
        alphaT = sb("alphaT", [40, KB * P], F32)
        ext_new = sb("ext_new", [40, 2], F32)
        ext = sb("ext", [40, 4], F32)
        ext_r = sb("ext_r", [H, 2], F32)
        shift = sb("shift", [H, 1], F32)

        psX = ps("psX", [P, 4, P], F32)
        psK = ps("psK", [P, 4, P], F32)
        psL = ps("psL", [P, F], F32)
        psA = ps("psA", [P, 512], F32)
        psM = [ps(f"psM{i}", [P, JB, P], BF16) for i in range(4)]
        alpha_nat = psA[:, 0:H]
        alpha_T = psA[0:40, P:2 * P]

        zeroed = sem("zeroed")
        consts = sem("consts")
        w_loaded = sem("w_loaded")
        dve_step = sem("dve_step")
        wa_ready = sem("wa_ready")
        adj_loaded = [sem(f"adj_loaded{i}") for i in range(2)]
        x_loaded = [sem(f"x_loaded{i}") for i in range(2)]
        x2_loaded = [sem(f"x2_loaded{i}") for i in range(2)]
        v_loaded = [sem(f"v_loaded{i}") for i in range(2)]
        compared = [sem(f"compared{i}") for i in range(2)]
        turned = [sem(f"turned{i}") for i in range(4)]
        mask_out = [sem(f"mask_out{i}") for i in range(4)]
        x_turned = [sem(f"x_turned{i}") for i in range(2)]
        x2_turned = [sem(f"x2_turned{i}") for i in range(2)]
        xT_ready = [sem(f"xT_ready{i}") for i in range(2)]
        xl_ready = sem("xl_ready")
        alpha_ready = [sem(f"alpha_ready{i}") for i in range(2)]
        kh_ready = sem("kh_ready")
        kl_ready = sem("kl_ready")
        kl_round = sem("kl_round")
        squared = [sem(f"squared{i}") for i in range(2)]
        reduced = sem("reduced")
        normed = sem("normed")
        xl_done = [sem(f"xl_done{i}") for i in range(2)]
        alpha_done = sem("alpha_done")
        summed = [sem(f"summed{i}") for i in range(2)]
        v_summed = [sem(f"v_summed{i}") for i in range(2)]
        xl_stored = [sem(f"xl_stored{i}") for i in range(2)]
        k_stored = sem("k_stored")
        tail_pe = sem("tail_pe")
        tail_dve = sem("tail_dve")
        al_stored = sem("al_stored")
        ext_step = sem("ext_step")
        shift_stored = sem("shift_stored")

        block = ctx.enter_context(nc.Block())
        UN = KB
        R = NT // UN

        @block.sync
        def _(sp):
            sp.dma_start(w_sb[:], W.rearrange("(k p) n -> p k n", p=P)).then_inc(w_loaded, 16)
            sp.dma_start(b_bc[:], b.partition_broadcast(P)).then_inc(w_loaded, 16)
            sp.dma_start(att_bc[:, 0, :], att_l.rearrange("h c -> (h c)").partition_broadcast(P)).then_inc(w_loaded, 16)
            sp.dma_start(att_bc[:, 1, :], att_r.rearrange("h c -> (h c)").partition_broadcast(P)).then_inc(w_loaded, 16)
            with sp.Fori(0, R) as r:
                for s in range(UN):
                    k, t, m = s % 2, r * UN + s, r * (UN // 2) + s // 2
                    rows = ds(t * P, P)
                    sp.wait_ge(x_turned[k], m)
                    sp.dma_start(x_sb[:, k, :], x[rows, :]).then_inc(x_loaded[k], 16)
                    sp.wait_ge(x2_turned[k], m)
                    sp.wait_ge(squared[k], m)
                    sp.dma_start(x2_sb[:, k, :], x2[rows, :]).then_inc(x2_loaded[k], 16)
                    sp.wait_ge(v_summed[k], m)
                    sp.dma_start(v_sb[:, k, :], v[rows, :]).then_inc(v_loaded[k], 16)
                    for bank in range(4):
                        sp.wait_ge(compared[bank % 2], t * 2 + bank // 2)
                        sp.dma_start(adj_sb[:, bank % 2, :], adj[rows, bank * QN:(bank + 1) * QN]
                                     ).then_inc(adj_loaded[bank % 2], 16)

        @block.gpsimd
        def _(pool):
            pool.memset(identF[:], 0.0).then_inc(zeroed, 1)
            pool.memset(identB[:], 0.0).then_inc(zeroed, 1)
            pool.memset(headmask[:], 1.0).then_inc(zeroed, 1)
            pool.memset(onesF[:], 1.0).then_inc(consts, 1)
            pool.wait_ge(zeroed, 3)
            for ident in (identF, identB):
                pool.affine_select(out=ident[:], in_=ident[:], compare_op=ALU.not_equal, fill=1.0, base=0,
                                   pattern=[[-1, P]], channel_multiplier=1).then_inc(consts, 1)
            pool.affine_select(out=headmask[:], in_=headmask[:], compare_op=ALU.is_ge, fill=0.0, base=0,
                               pattern=[[1, F]], channel_multiplier=-C).then_inc(zeroed, 1)
            pool.wait_ge(zeroed, 4)
            pool.affine_select(out=headmask[:], in_=headmask[:], compare_op=ALU.is_ge, fill=0.0, base=C - 1,
                               pattern=[[-1, F]], channel_multiplier=C).then_inc(consts, 1)
            pool.memset(xl_sum[:], 0.0).then_inc(consts, 1)
            pool.memset(v_sum[:], 0.0).then_inc(consts, 1)
            pool.wait_ge(consts, 6)
            with pool.Fori(0, R) as r:
                for s in range(UN):
                    k, m = s % 2, r * (UN // 2) + s // 2
                    t = r * UN + s
                    pool.wait_ge(x2_loaded[k], m * 16 + 16)
                    pool.wait_ge(reduced, t)
                    pool.tensor_tensor(sq[:], x2_sb[:, k, :], x2_sb[:, k, :], ALU.mult).then_inc(squared[k], 1)
                    pool.wait_ge(v_loaded[k], m * 16 + 16)
                    if k == 1:
                        pool.wait_ge(v_summed[0], m + 1)
                    else:
                        pool.wait_ge(v_summed[1], m)
                    pool.tensor_tensor(v_sum[:], v_sum[:], v_sb[:, k, :], ALU.add).then_inc(v_summed[k], 1)
                    pool.wait_ge(xl_done[k], m * 2 + 2)
                    if k == 1:
                        pool.wait_ge(summed[0], m + 1)
                    else:
                        pool.wait_ge(summed[1], m)
                    pool.tensor_tensor(xl_sum[:].rearrange("p (a c) -> p a c", a=PAIRS),
                                       xl_sum[:].rearrange("p (a c) -> p a c", a=PAIRS),
                                       xl_sb[:, k, :, 0:2 * C], ALU.add).then_inc(summed[k], 1)
                    pool.dma_start(xl_dram[ds(t * P, P), :, :], xl_sb[:, k, :, :]).then_inc(xl_stored[k], 16)
                pool.wait_ge(kl_ready, r * UN + UN)
                for part, kk in enumerate((kh, kl)):
                    pool.dma_start(k_dram[part].rearrange("(a p) n -> p a n", p=P)[:, :, ds(r * (KB * P), KB * P)],
                                   kk[:]).then_inc(k_stored, 16)
                pool.wait_ge(alpha_done, r * UN + UN)
                pool.dma_start(al_dram[:, ds(r * (KB * P), KB * P)], alphaT[0:H, :]).then_inc(al_stored, 16)
            pool.wait_ge(tail_dve, 1)
            pool.dma_start(shift_dram[0].rearrange("(h o) -> h o", o=1), shift[:]).then_inc(shift_stored, 16)
            pool.wait_ge(shift_stored, 16)
            pool.wait_ge(al_stored, 16 * R)
            pool.wait_ge(k_stored, 32 * R)
            for k in range(2):
                pool.wait_ge(xl_stored[k], 16 * (NT // 2))

        @block.scalar
        def _(act):
            with act.Fori(0, R) as r:
                for s in range(UN):
                    k, t, m = s % 2, r * UN + s, r * (UN // 2) + s // 2
                    act.wait_ge(x_turned[k], m + 1)
                    act.wait_ge(alpha_ready[k], m)
                    nc.scalar.activation(xT[:, k, :, :], psX[:], ACT.Copy).then_inc(xT_ready[k], 1)
                    act.wait_ge(x2_turned[k], m + 1)
                    if s == 0:
                        act.wait_ge(k_stored, r * 32)
                    nc.scalar.activation(kh[:, :, s * P:(s + 1) * P], psK[:], ACT.Copy).then_inc(kh_ready, 1)
                    for bank in range(3):
                        act.wait_ge(turned[bank], t + 1)
                        nc.scalar.activation(maskT[:, bank * JB:(bank + 1) * JB, ds(t * P, P)], psM[bank][:],
                                             ACT.Copy).then_inc(mask_out[bank], 1)

        @block.tensor
        def _(pe):
            pe.wait_ge(consts, 6)
            pe.wait_ge(wa_ready, 1)
            with pe.Fori(0, R) as r:
                for s in range(UN):
                    k, t, m = s % 2, r * UN + s, r * (UN // 2) + s // 2
                    pe.wait_ge(x_loaded[k], m * 16 + 16)
                    if k == 1:
                        pe.wait_ge(xT_ready[0], m + 1)
                    else:
                        pe.wait_ge(xT_ready[1], m)
                    for c in range(4):
                        last = nc.tensor.transpose(psX[:, c, :], x_sb[:, k, c * P:(c + 1) * P], identF[:])
                    last.then_inc(x_turned[k], 1)
                    pe.wait_ge(x2_loaded[k], m * 16 + 16)
                    pe.wait_ge(kl_ready, t)
                    for c in range(4):
                        last = nc.tensor.transpose(psK[:, c, :], x2_sb[:, k, c * P:(c + 1) * P], identF[:])
                    last.then_inc(x2_turned[k], 1)
                    pe.wait_ge(xT_ready[k], m + 1)
                    if k == 1:
                        pe.wait_ge(xl_done[0], m * 2 + 2)
                    else:
                        pe.wait_ge(xl_done[1], m * 2)
                    for c in range(4):
                        last = nc.tensor.matmul(psL[:], xT[:, k, c, :], w_sb[:, c, :], start=(c == 0), stop=(c == 3))
                    last.then_inc(xl_ready, 1)
                    pe.wait_ge(alpha_done, t)
                    for c in range(4):
                        nc.tensor.matmul(alpha_nat, xT[:, k, c, :], wa[:, c, 32:40], start=(c == 0), stop=False)
                    nc.tensor.matmul(alpha_nat, onesF[0:1, :], ba[0:1, 32:40], start=False, stop=True)
                    for c in range(4):
                        nc.tensor.matmul(alpha_T, wa[:, c, :], xT[:, k, c, :], start=(c == 0), stop=False)
                    nc.tensor.matmul(alpha_T, ba[0:1, :], onesF[0:1, :], start=False,
                                     stop=True).then_inc(alpha_ready[k], 1)
                    for bank in range(4):
                        pe.wait_ge(compared[bank % 2], t * 2 + bank // 2 + 1)
                        pe.wait_ge(mask_out[bank], t)
                        for c in range(JB):
                            last = nc.tensor.transpose(psM[bank][:, c, :], mask_sb[:, bank % 2, c * P:(c + 1) * P],
                                                       identB[:])
                        last.then_inc(turned[bank], 1)
            for k in range(2):
                pe.wait_ge(summed[k], NT // 2)
                pe.wait_ge(v_summed[k], NT // 2)
            pe.wait_ge(kl_ready, NT)
            pe.wait_ge(xl_done[1], NT)
            nc.tensor.matmul(psL[0:H, :], onesF[:, 0:H], xl_sum[:], start=True, stop=True).then_inc(tail_pe, 1)
            nc.tensor.matmul(psK[0:H, :, :].rearrange("p a c -> p (a c)"), onesF[:, 0:H], v_sum[:],
                             start=True, stop=True).then_inc(tail_pe, 1)
            pe.wait_ge(normed, NT)
            nc.tensor.transpose(psX[0:H, 0, :], norm_max[:], identF[:]).then_inc(tail_pe, 1)

        @block.vector
        def _(dve):
            steps = [0]

            def then(ins):
                steps[0] += 1
                ins.then_inc(dve_step, 1)
                dve.wait_ge(dve_step, steps[0])

            nc.vector.memset(wa[:], 0.0)
            nc.vector.memset(norm_max[:], 0.0)
            then(nc.vector.memset(ba[:], 0.0))
            dve.wait_ge(w_loaded, 64)
            for a in range(2):
                for c in range(5):
                    src = w_sb[:, c, :] if c < 4 else b_bc[:]
                    dst = wa[:, c, 32 * a:32 * a + H] if c < 4 else ba[:, 32 * a:32 * a + H]
                    then(nc.vector.tensor_tensor(wa_tmp[:], src, att_bc[:, a, :], ALU.mult))
                    then(nc.vector.tensor_reduce(dst, wa_tmp[:].rearrange("p (h c) -> p h c", h=H), AX.X, ALU.add))
            nc.vector.memset(ext[:], 0.0).then_inc(wa_ready, 1)
            with dve.Fori(0, R) as r:
                for s in range(UN):
                    k, t, m = s % 2, r * UN + s, r * (UN // 2) + s // 2
                    for bank in range(4):
                        dve.wait_ge(adj_loaded[bank % 2], t * 32 + (bank // 2) * 16 + 16)
                        dve.wait_ge(turned[(bank + 2) % 4], t + (1 if bank >= 2 else 0))
                        nc.vector.tensor_scalar(mask_sb[:, bank % 2, :], adj_sb[:, bank % 2, :], 0.0, None,
                                                ALU.is_gt).then_inc(compared[bank % 2], 1)
                    dve.wait_ge(kh_ready, t + 1)
                    nc.vector.tensor_tensor(kl[:, :, s * P:(s + 1) * P], psK[:], kh[:, :, s * P:(s + 1) * P],
                                            ALU.subtract).then_inc(kl_ready, 1)
                    dve.wait_ge(squared[k], m + 1)
                    dve.wait_ge(normed, t)
                    nc.vector.tensor_reduce(norms[:], sq[:].rearrange("p (h c) -> p h c", h=H), AX.X,
                                            ALU.add).then_inc(reduced, 1)
                    dve.wait_ge(xl_ready, t + 1)
                    dve.wait_ge(xl_stored[k], m * 16)
                    dve.wait_ge(summed[k], m)
                    nc.vector.tensor_tensor(xl_sb[:, k, :, 0:2 * C], psL[:].rearrange("p (a c) -> p a c", a=PAIRS),
                                            b_bc[:].rearrange("p (a c) -> p a c", a=PAIRS),
                                            ALU.add).then_inc(xl_done[k], 1)
                    dve.wait_ge(reduced, t + 1)
                    nc.vector.tensor_tensor(norm_max[:], norm_max[:], norms[:], ALU.max).then_inc(normed, 1)
                    dve.wait_ge(alpha_ready[k], m + 1)
                    nc.vector.tensor_copy(xl_sb[:, k, :, 2 * C:XW],
                                          alpha_nat.rearrange("p (a h) -> p a h", h=2)).then_inc(xl_done[k], 1)
                    if s == 0:
                        dve.wait_ge(al_stored, r * 16)
                    nc.vector.tensor_copy(alphaT[:, s * P:(s + 1) * P], alpha_T).then_inc(alpha_done, 1)
                    dve.wait_ge(turned[3], t + 1)
                    nc.vector.tensor_copy(maskT[:, 3 * JB:4 * JB, ds(t * P, P)], psM[3][:]).then_inc(mask_out[3], 1)
                dve.wait_ge(alpha_done, r * UN + UN)
                for i, op in enumerate((ALU.max, ALU.min)):
                    nc.vector.tensor_reduce(ext_new[:, i:i + 1], alphaT[:], AX.X, op).then_inc(ext_step, 1)
                dve.wait_ge(ext_step, r * 4 + 2)
                for i, op in enumerate((ALU.max, ALU.min)):
                    nc.vector.tensor_tensor(ext[:, i:i + 1], ext[:, i:i + 1], ext_new[:, i:i + 1], op).then_inc(ext_step, 1)
                dve.wait_ge(ext_step, r * 4 + 4)
            then(nc.vector.tensor_scalar(ext[:, 2:3], ext[:, 1:2], -1.0, None, ALU.mult))
            then(nc.vector.tensor_tensor(ext[:, 3:4], ext[:, 0:1], ext[:, 2:3], ALU.max))
            then(nc.vector.tensor_copy(ext_r[:, 0:1], ext[32:40, 3:4]))
            then(nc.vector.tensor_tensor(ext_r[:, 1:2], ext[0:H, 3:4], ext_r[:, 0:1], ALU.mult))
            nc.vector.tensor_scalar(shift[:], ext_r[:, 1:2], -1.0, None, ALU.mult).then_inc(tail_dve, 1)
            dve.wait_ge(tail_pe, 1)
            nc.vector.tensor_tensor(colsum[:, 0, :], psL[0:H, :], headmask[:], ALU.mult)
            dve.wait_ge(tail_pe, 2)
            nc.vector.tensor_tensor(colsum[:, 1, :], psK[0:H, :, :].rearrange("p a c -> p (a c)"), headmask[:], ALU.mult)
            dve.wait_ge(tail_pe, 3)
            then(nc.vector.tensor_reduce(kmax[:], psX[0:H, 0, :], AX.X, ALU.max))


def attend_gat(nc, keep, xl_dram, al_dram, shift_dram, o_dram, d_dram, maskT, onesF):
    clear = clear_with(nc)
    ctx = ExitStack()
    with ctx:
        def sb(name, shape, dt):
            return ctx.enter_context(nc.sbuf_tensor(name, shape, dt))

        def ps(name, shape, dt):
            return ctx.enter_context(nc.psum_tensor(name, shape, dt))

        def sem(name):
            return keep.enter_context(nc.semaphore(name))

        al_bc = sb("al_bc", [P, 2, 2, IC], F32)
        shift_bc = sb("g_shift", [P, 2, 2], F32)
        xl = sb("g_xl", [P, 2, KB, XW], F32)
        w = sb("g_weights", [P, NP, 2, IC], F32)
        total = sb("g_total", [P, 2, IC], F32)
        o_sb = sb("g_o", [P, 2, IC], F32)
        d_sb = sb("g_d", [P, 2, HALF], F32)
        psO = [ps(f"g_psO{i}", [P, 2, HALF], F32) for i in range(2)]
        psD = [ps(f"g_psD{i}", [P, HALF], F32) for i in range(2)]
        zeros = sb("g_zeros", [1, HALF], BF16)
        zeros_set = sem("g_zeros_set")

        const_loaded = [sem(f"g_const_loaded{i}") for i in range(2)]
        const_used = [sem(f"g_const_used{i}") for i in range(2)]
        xl_loaded = [sem(f"g_xl_loaded{i}") for i in range(2)]
        exped = sem("g_exped")
        masked = sem("g_masked")
        w_used = [sem(f"g_w_used{u}") for u in range(JB)]
        added = sem("g_added")
        total_used = sem("g_total_used")
        cleared = sem("g_cleared")
        evacuated = [sem(f"g_evacuated{i}") for i in range(2)]
        stored = [sem(f"g_stored{i}") for i in range(2)]

        block = ctx.enter_context(nc.Block())

        @block.sync
        def _(sp):
            with sp.Fori(0, CHUNKS) as ic:
                with sp.Fori(0, PAIRS // 2) as pp:
                    for par in range(2):
                        pair, use = pp * 2 + par, ic * (PAIRS // 2) + pp
                        sp.wait_ge(const_used[par], use)
                        sp.dma_start(al_bc[:, par, :, :],
                                     al_dram[ds(pair * 2, 2), ds(ic * IC, IC)].partition_broadcast(P)
                                     ).then_inc(const_loaded[par], 16)
                        sp.dma_start(shift_bc[:, par, :],
                                     shift_dram[0, ds(pair * 2, 2)].partition_broadcast(P)
                                     ).then_inc(const_loaded[par], 16)
                        with sp.Fori(0, NB) as q:
                            for slot in range(2):
                                B = (use * 2 + par) * NB + q
                                sp.wait_ge(w_used[slot * KB + KB - 1], B)
                                sp.dma_start(xl[:, slot, :, :],
                                             xl_dram[ds(q * (JB * P) + slot * (KB * P), KB * P), ds(pair, 1), :]
                                             .rearrange("(t p) a c -> p (t a) c", p=P)).then_inc(xl_loaded[slot], 16)

        FIRST, SECOND = 2, 3
        GG = CHUNKS * PAIRS // 2

        @block.scalar
        def _(act):
            def weights(gg, par, B, u):
                slot = u // KB
                if u % KB == 0:
                    act.wait_ge(xl_loaded[slot], B * 16 + 16)
                wait_buffer(act, w_used, B, u)
                if u - NP in (FIRST, SECOND):
                    act.wait_ge(added, B + 1)
                for h in range(2):
                    nc.scalar.activation(w[:, u % NP, h, :], al_bc[:, par, h, :], ACT.Exp,
                                         bias=shift_bc[:, par, h:h + 1],
                                         scale=xl[:, slot, u % KB, 2 * C + h:2 * C + h + 1]).then_inc(exped, 1)

            def evacuate(groups, par):
                act.wait_ge(w_used[JB - 1], groups * NB)
                nc.scalar.activation(o_sb[:, par, :], psO[par][:].rearrange("p a c -> p (a c)"), ACT.Copy
                                     ).then_inc(evacuated[par], 1)
                nc.scalar.activation(d_sb[:, par, :], psD[par][:], ACT.Copy).then_inc(evacuated[par], 1)

            act.wait_ge(cleared, 1)
            with act.Fori(0, GG) as gg:
                for par in range(2):
                    G = gg * 2 + par
                    act.wait_ge(const_loaded[par], gg * 32 + 32)
                    for u in range(JB):
                        weights(gg, par, G * NB, u)
                        if u == 1:
                            evacuate(G, 1 - par)
                    with act.Fori(1, NB) as q:
                        for u in range(JB):
                            weights(gg, par, G * NB + q, u)
                    act.wait_ge(exped, (G + 1) * (2 * NT))
                    act.sem_inc(const_used[par], 1)
                    act.wait_ge(stored[par], gg * 48)
            evacuate(2 * GG, 1)

        @block.vector
        def _(dve):
            with dve.Fori(0, CHUNKS) as ic:
                with dve.Fori(0, PAIRS) as pair:
                    with dve.Fori(0, NB) as q:
                        B = (ic * PAIRS + pair) * NB + q
                        for u in range(JB):
                            for h in range(2):
                                dve.wait_ge(exped, (B * JB + u) * 2 + h + 1)
                                nc.vector.tensor_tensor(w[:, u % NP, h, :], w[:, u % NP, h, :],
                                                        maskT[:, ds(q * JB + u, 1), ds(ic * IC, IC)]
                                                        .rearrange("p a c -> p (a c)"),
                                                        ALU.mult).then_inc(masked, 1)
                            if u == SECOND + 1:
                                dve.wait_ge(total_used, B)
                                dve.wait_ge(masked, (B * JB + SECOND) * 2 + 2)
                                nc.vector.tensor_tensor(total[:], w[:, FIRST % NP, :, :], w[:, SECOND % NP, :, :],
                                                        ALU.add).then_inc(added, 1)

        @block.tensor
        def _(pe):
            pe.wait_ge(zeros_set, 1)
            clear(psO[1], psD[1], zeros).then_inc(cleared, 1)
            with pe.Fori(0, GG) as gg:
                for par in range(2):
                    pe.wait_ge(evacuated[par], gg * 2 + 2 * par)
                    clear(psO[par], psD[par], zeros)
                    with pe.Fori(0, NB) as q:
                        B = (gg * 2 + par) * NB + q
                        for u in range(JB):
                            n, slot = B * JB + u, u // KB
                            pe.wait_ge(xl_loaded[slot], B * 16 + 16)
                            pe.wait_ge(masked, n * 2 + 2)
                            last = add_values(nc, w[:, u % NP, :, :], xl[:, slot, u % KB, 0:2 * C], psO[par])
                            if u not in (FIRST, SECOND):
                                last = add_weights(nc, w[:, u % NP, :, :], psD[par], onesF)
                            last.then_inc(w_used[u], 1)
                            if u == SECOND + 1:
                                pe.wait_ge(added, B + 1)
                                add_weights(nc, total, psD[par], onesF).then_inc(total_used, 1)

        @block.gpsimd
        def _(pool):
            pool.memset(zeros[:], 0.0).then_inc(zeros_set, 1)
            store_groups(pool, 0, 1, o_sb, d_sb, evacuated, stored, o_dram, d_dram)


def clear_with(nc):
    def clear(psO, psD, zeros):
        for bank in (psO[:, 0, :], psO[:, 1, :], psD[:]):
            last = nc.tensor.matmul(bank, zeros[0:1, 0:P], zeros[0:1, :], start=True, stop=False, skip_group_check=True)
        return last
    return clear


def add_values(nc, w, values, psO):
    for hf in range(2):
        for h in range(2):
            last = nc.tensor.matmul(psO[h * C:(h + 1) * C, hf, :], values[:, h * C:(h + 1) * C],
                                    w[:, h, hf * HALF:(hf + 1) * HALF], start=False, stop=False, skip_group_check=True)
    return last


def add_weights(nc, w, psD, onesF):
    for hf in range(2):
        for h in range(2):
            row = 32 * (2 * h + hf)
            last = nc.tensor.matmul(psD[row:row + 32, :], onesF[:, 0:32], w[:, h, hf * HALF:(hf + 1) * HALF],
                                    start=False, stop=False, skip_group_check=True)
    return last


def wait_buffer(act, w_used, B, u):
    if u >= NP:
        act.wait_ge(w_used[u - NP], B + 1)
    else:
        act.wait_ge(w_used[u + JB - NP], B)


def store_groups(pool, layer, unstored, o_sb, d_sb, evacuated, stored, o_dram, d_dram):
    with pool.Fori(0, CHUNKS) as ic:
        with pool.Fori(0, PAIRS // 2) as pp:
            for par in range(2):
                pair, use = pp * 2 + par, ic * (PAIRS // 2) + pp
                pool.wait_ge(evacuated[par], use * 2 + 2 + 2 * unstored * par)
                pool.dma_start(o_dram[layer, ds(pair, 1), :, ds(ic * IC, IC)].rearrange("a p n -> (a p) n"),
                               o_sb[:, par, :]).then_inc(stored[par], 16)
                for hf in range(2):
                    pool.dma_start(d_dram[layer, ds(pair * 2, 2), ds(ic * IC + hf * HALF, HALF)],
                                   d_sb[32 * hf:P:64, par, :]).then_inc(stored[par], 16)
    for par in range(2):
        pool.wait_ge(stored[par], 48 * CHUNKS * PAIRS // 2)


def finish_layer(nc, keep, layer, x, o_dram, d_dram, result, q_dram, shift_dram, identF, colsum, kmax):
    first = layer == 0
    ctx = ExitStack()
    with ctx:
        def sb(name, shape, dt):
            return ctx.enter_context(nc.sbuf_tensor(f"f{layer}_{name}", shape, dt))

        def ps(name, shape, dt):
            return ctx.enter_context(nc.psum_tensor(f"f{layer}_{name}", shape, dt))

        def sem(name):
            return keep.enter_context(nc.semaphore(f"f{layer}_{name}"))

        T = 4
        R = NT // T
        oT = sb("oT", [P, PAIRS, T * P], F32)
        xin = sb("xin", [P, T, F], F32)
        dT = sb("dT", [H, N], F32)
        alone = sb("alone", [H, T, P], F32)
        den = sb("den", [H, T, P], F32)
        rden = sb("rden", [P, T, H], F32)
        y = sb("y", [P, F], F32)
        z = sb("z", [P, T, F], F32)
        stats = sb("stats", [P, T, 6], F32)
        mv = sb("mv", [P, T, 2], F32)
        std = sb("std", [P, T], F32)
        rstd = sb("rstd", [P, T], F32)
        res = sb("res", [P, T, F], F32)
        eps = sb("eps", [P, 1], F32)
        psO = [ps(f"psO{i}", [P, F], F32) for i in range(2)]
        psR = [ps(f"psR{i}", [P, H], F32) for i in range(2)]

        eps_set = sem("eps_set")
        o_loaded = sem("o_loaded")
        d_loaded = sem("d_loaded")
        x_loaded = sem("x_loaded")
        alone_set = sem("alone_set")
        den_ready = sem("den_ready")
        turned = sem("turned")
        chain = sem("chain")
        added = sem("added")
        stats_seen = sem("stats_seen")
        var_ready = sem("var_ready")
        std_ready = sem("std_ready")
        rstd_ready = sem("rstd_ready")
        res_ready = sem("res_ready")
        res_stored = sem("res_stored")
        if first:
            qh = sb("qh", [P, PAIRS, T * P], F16)
            ql = sb("ql", [P, PAIRS, T * P], F16)
            sq = sb("sq", [P, T, F], F32)
            norms = sb("norms", [P, T * H], F32)
            norm_max = sb("norm_max", [P, T * H], F32)
            norm_all = sb("norm_all", [P, H], F32)
            qmax = sb("qmax", [H, 4], F32)
            psQ = [ps(f"psQ{i}", [P, PAIRS, P], F32) for i in range(T)]
            q_turned = sem("q_turned")
            qh_ready = sem("qh_ready")
            ql_ready = sem("ql_ready")
            squared = sem("squared")
            reduced = sem("reduced")
            normed = sem("normed")
            q_stored = sem("q_stored")
            tail = sem("tail")
            s_stored = sem("s_stored")

        block = ctx.enter_context(nc.Block())

        @block.sync
        def _(sp):
            sp.dma_start(dT[:], d_dram[layer]).then_inc(d_loaded, 16)
            with sp.Fori(0, R) as r:
                rows = ds(r * (T * P), T * P)
                sp.wait_ge(turned, r * T)
                sp.dma_start(oT[:], o_dram[layer, :, :, rows].rearrange("a p n -> p a n")).then_inc(o_loaded, 16)
                sp.wait_ge(added, r * T)
                sp.dma_start(xin[:], x[rows, :].rearrange("(t p) c -> p t c", p=P)).then_inc(x_loaded, 16)

        @block.tensor
        def _(pe):
            with pe.Fori(0, R) as r:
                pe.wait_ge(o_loaded, r * 16 + 16)
                pe.wait_ge(den_ready, r + 1)
                for s in range(T):
                    t = r * T + s
                    if s < 2:
                        pe.wait_ge(added, r * T)
                    else:
                        pe.wait_ge(added, t - 1)
                    for a in range(PAIRS):
                        nc.tensor.matmul(psO[s % 2][:, a * P:(a + 1) * P], oT[:, a, s * P:(s + 1) * P], identF[:],
                                         start=(a == 0), stop=False, skip_group_check=True)
                    nc.tensor.matmul(psO[s % 2][:], alone[:, s, :], colsum[:, layer, :], start=False, stop=True,
                                     skip_group_check=True)
                    nc.tensor.matmul(psR[s % 2][:], den[:, s, :], identF[0:H, 0:H], start=True, stop=True
                                     ).then_inc(turned, 1)
                if first:
                    for s in range(T):
                        pe.wait_ge(res_ready, r * T + s + 1)
                        pe.wait_ge(ql_ready, r * T)
                        for a in range(PAIRS):
                            last = nc.tensor.transpose(psQ[s][:, a, :], res[:, s, a * P:(a + 1) * P], identF[:])
                        last.then_inc(q_turned, 1)
            if first:
                pe.wait_ge(tail, 1)
                pe.wait_ge(added, NT)
                nc.tensor.transpose(psO[0][0:H, 0:P], norm_all[:], identF[:]).then_inc(tail, 1)

        @block.scalar
        def _(act):
            act.wait_ge(eps_set, 1)
            with act.Fori(0, R) as r:
                act.wait_ge(var_ready, r * T + T)
                act.wait_ge(rstd_ready, r)
                nc.scalar.activation(std[:], mv[:, :, 1], ACT.Sqrt, bias=eps[:]).then_inc(std_ready, 1)
                if first:
                    for s in range(T):
                        act.wait_ge(q_turned, r * T + s + 1)
                        if s == 0:
                            act.wait_ge(q_stored, r * 32)
                        nc.scalar.activation(qh[:, :, s * P:(s + 1) * P], psQ[s][:], ACT.Copy).then_inc(qh_ready, 1)
                else:
                    act.wait_ge(res_ready, r * T + T)
                act.dma_start(result[ds(r * (T * P), T * P), :].rearrange("(t p) c -> p t c", p=P), res[:]
                              ).then_inc(res_stored, 16)
            if first:
                act.wait_ge(tail, 4)
                nc.scalar.activation(qmax[:, 2:3], qmax[:, 1:2], ACT.Sqrt).then_inc(tail, 1)
            act.wait_ge(res_stored, 16 * R)

        @block.gpsimd
        def _(pool):
            if first:
                with pool.Fori(0, R) as r:
                    for s in range(T):
                        pool.wait_ge(res_ready, r * T + s + 1)
                        pool.wait_ge(reduced, r)
                        pool.tensor_tensor(sq[:, s, :], res[:, s, :], res[:, s, :], ALU.mult).then_inc(squared, 1)
                    pool.wait_ge(ql_ready, r * T + T)
                    for part, qq in enumerate((qh, ql)):
                        pool.dma_start(q_dram[part].rearrange("(a p) n -> p a n", p=P)[:, :, ds(r * (T * P), T * P)],
                                       qq[:]).then_inc(q_stored, 16)
                pool.wait_ge(tail, 6)
                pool.dma_start(shift_dram[1].rearrange("(h o) -> h o", o=1), qmax[:, 3:4]).then_inc(s_stored, 16)
                pool.wait_ge(s_stored, 16)
                pool.wait_ge(q_stored, 32 * R)

        @block.vector
        def _(dve):
            nc.vector.memset(eps[:], EPS).then_inc(eps_set, 1)
            if first:
                nc.vector.memset(norm_max[:], 0.0)
            dve.wait_ge(d_loaded, 16)
            LINKS = 3 * T
            with dve.Fori(0, R) as r:
                part = ds(r * (T * P), T * P)
                dve.wait_ge(turned, r * T)
                nc.vector.tensor_scalar(alone[:].rearrange("h t p -> h (t p)"), dT[:, part], 0.0, None,
                                        ALU.is_equal).then_inc(alone_set, 1)
                dve.wait_ge(alone_set, r + 1)
                nc.vector.scalar_tensor_tensor(out=den[:].rearrange("h t p -> h (t p)"),
                                               in0=alone[:].rearrange("h t p -> h (t p)"), scalar=float(N),
                                               in1=dT[:, part], op0=ALU.mult, op1=ALU.add).then_inc(den_ready, 1)
                for s in range(T):
                    t = r * T + s
                    dve.wait_ge(turned, t + 1)
                    nc.vector.reciprocal(rden[:, s, :], psR[s % 2][:]).then_inc(chain, 1)
                    dve.wait_ge(chain, r * LINKS + 3 * s + 1)
                    nc.vector.tensor_tensor(y[:].rearrange("p (h c) -> p h c", h=H),
                                            psO[s % 2][:].rearrange("p (h c) -> p h c", h=H),
                                            rden[:, s, :].unsqueeze(2).to_broadcast([P, H, C]), ALU.mult
                                            ).then_inc(chain, 1)
                    if s == 0:
                        dve.wait_ge(x_loaded, r * 16 + 16)
                    dve.wait_ge(chain, r * LINKS + 3 * s + 2)
                    if first:
                        ins = nc.vector.scalar_tensor_tensor(out=z[:, s, :], in0=y[:], scalar=0.0,
                                                             in1=xin[:, s, :], op0=ALU.max, op1=ALU.add)
                    else:
                        ins = nc.vector.tensor_tensor(z[:, s, :], y[:], xin[:, s, :], ALU.add)
                    ins.then_inc(added, 1)
                    dve.wait_ge(added, t + 1)
                    nc.vector.bn_stats(stats[:, s, :], z[:, s, :]).then_inc(chain, 1)
                    dve.wait_ge(chain, r * LINKS + 3 * s + 3)
                    dve.sem_inc(stats_seen, 1)
                    nc.vector.bn_aggr(mv[:, s, :], stats[:, s, :]).then_inc(var_ready, 1)
                dve.wait_ge(std_ready, r + 1)
                nc.vector.reciprocal(rstd[:], std[:]).then_inc(rstd_ready, 1)
                dve.wait_ge(rstd_ready, r + 1)
                dve.wait_ge(res_stored, r * 16)
                for s in range(T):
                    nc.vector.tensor_scalar(res[:, s, :], z[:, s, :], mv[:, s, 0:1], rstd[:, s:s + 1],
                                            ALU.subtract, ALU.mult).then_inc(res_ready, 1)
                if first:
                    for s in range(T):
                        dve.wait_ge(qh_ready, r * T + s + 1)
                        nc.vector.tensor_tensor(ql[:, :, s * P:(s + 1) * P], psQ[s][:], qh[:, :, s * P:(s + 1) * P],
                                                ALU.subtract).then_inc(ql_ready, 1)
                    dve.wait_ge(squared, r * T + T)
                    nc.vector.tensor_reduce(norms[:], sq[:].rearrange("p t (h c) -> p (t h) c", h=H), AX.X, ALU.add
                                            ).then_inc(reduced, 1)
                    dve.wait_ge(reduced, r + 1)
                    nc.vector.tensor_tensor(norm_max[:], norm_max[:], norms[:], ALU.max).then_inc(normed, 1)
            if first:
                dve.wait_ge(normed, R)
                nc.vector.tensor_reduce(norm_all[:], norm_max[:].rearrange("p (t h) -> p h t", h=H), AX.X, ALU.max
                                        ).then_inc(tail, 1)
                dve.wait_ge(tail, 2)
                nc.vector.tensor_reduce(qmax[:, 0:1], psO[0][0:H, 0:P], AX.X, ALU.max).then_inc(tail, 1)
                dve.wait_ge(tail, 3)
                nc.vector.tensor_tensor(qmax[:, 1:2], qmax[:, 0:1], kmax[:], ALU.mult).then_inc(tail, 1)
                dve.wait_ge(tail, 5)
                nc.vector.tensor_scalar(qmax[:, 3:4], qmax[:, 2:3], -SCALE, None, ALU.mult).then_inc(tail, 1)


def attend_dot(nc, keep, v, q_dram, k_dram, shift_dram, o_dram, d_dram, maskT, onesF):
    clear = clear_with(nc)
    ctx = ExitStack()
    with ctx:
        def sb(name, shape, dt):
            return ctx.enter_context(nc.sbuf_tensor(f"a_{name}", shape, dt))

        def ps(name, shape, dt):
            return ctx.enter_context(nc.psum_tensor(f"a_{name}", shape, dt))

        def sem(name):
            return keep.enter_context(nc.semaphore(f"a_{name}"))

        q_sb = sb("q", [P, 2, 2, 2, IC], F16)
        shift_bc = sb("shift", [P, 2, 2], F32)
        k_sb = sb("k", [P, 2, 2, KB * P], F16)
        v_sb = sb("v", [P, 2, KB, 2 * C], F32)
        w = sb("weights", [P, NP, 2, IC], F32)
        acc = sb("set_total", [P, 2, 2, IC], F32)
        o_sb = sb("o", [P, 2, IC], F32)
        d_sb = sb("d", [P, 2, HALF], F32)
        zeros = sb("zeros", [1, HALF], BF16)
        psS = [ps(f"psS{i}", [P, 2, HALF], F32) for i in range(2)]
        psO = ps("psO", [P, 2, HALF], F32)
        psD = ps("psD", [P, HALF], F32)

        zeros_set = sem("zeros_set")
        q_loaded = [sem(f"q_loaded{i}") for i in range(2)]
        k_loaded = [sem(f"k_loaded{i}") for i in range(2)]
        v_loaded = [sem(f"v_loaded{i}") for i in range(2)]
        scored = [[sem(f"scored{h}_{slot}") for slot in range(2)] for h in range(2)]
        exped = [sem(f"exped{i}") for i in range(2)]
        masked = sem("masked")
        w_used = [sem(f"w_used{u}") for u in range(JB)]
        added = [sem(f"added{i}") for i in range(3)]
        total_used = [sem(f"total_used{i}") for i in range(3)]
        evacuated = [sem(f"evacuated{i}") for i in range(2)]
        stored = [sem(f"stored{i}") for i in range(2)]

        block = ctx.enter_context(nc.Block())
        GG = CHUNKS * PAIRS // 2

        @block.sync
        def _(sp):
            with sp.Fori(0, CHUNKS) as ic:
                with sp.Fori(0, PAIRS // 2) as pp:
                    for par in range(2):
                        pair, use = pp * 2 + par, ic * (PAIRS // 2) + pp
                        G = use * 2 + par
                        sp.wait_ge(evacuated[par], use * 2)
                        for twice in range(2):
                            for part in range(2):
                                sp.dma_start(q_sb[twice * C:(twice + 1) * C, par, part, :, :],
                                             q_dram[part, ds(pair * (2 * C), 2 * C), ds(ic * IC, IC)]
                                             .rearrange("(h c) n -> c h n", h=2)).then_inc(q_loaded[par], 16)
                        sp.dma_start(shift_bc[:, par, :], shift_dram[1, ds(pair * 2, 2)].partition_broadcast(P)
                                     ).then_inc(q_loaded[par], 16)
                        with sp.Fori(0, NB) as q:
                            for slot in range(2):
                                B = G * NB + q
                                src = q * (JB * P) + slot * (KB * P)
                                sp.wait_ge(scored[1][slot], B * KB)
                                for part in range(2):
                                    sp.dma_start(k_sb[part * C:(part + 1) * C, slot, :, :],
                                                 k_dram[part, ds(pair * (2 * C), 2 * C), ds(src, KB * P)]
                                                 .rearrange("(h c) n -> c h n", h=2)).then_inc(k_loaded[slot], 16)
                                sp.wait_ge(w_used[slot * KB + KB - 1], B)
                                sp.dma_start(v_sb[:, slot, :, :],
                                             v[ds(src, KB * P), ds(pair * (2 * C), 2 * C)]
                                             .rearrange("(t p) c -> p t c", p=P)).then_inc(v_loaded[slot], 16)

        @block.tensor
        def _(pe):
            def scores(B, u, par):
                n, slot = B * JB + u, u // KB
                if u % KB == 0:
                    pe.wait_ge(k_loaded[slot], B * 32 + 32)
                for h in range(2):
                    pe.wait_ge(exped[h], n)
                    for hf in range(2):
                        for part in range(2):
                            last = nc.tensor.matmul(psS[h][:, hf, :],
                                                    k_sb[:, slot, h, (u % KB) * P:(u % KB + 1) * P],
                                                    q_sb[:, par, part, h, hf * HALF:(hf + 1) * HALF],
                                                    start=(part == 0), stop=(part == 1))
                    last.then_inc(scored[h][slot], 1)

            def values(B, u):
                n, slot = B * JB + u, u // KB
                if u % KB == 0:
                    pe.wait_ge(v_loaded[slot], B * 16 + 16)
                pe.wait_ge(masked, n * 2 + 2)
                add_values(nc, w[:, u % NP, :, :], v_sb[:, slot, u % KB, :], psO).then_inc(w_used[u], 1)

            def weights(B, i):
                pe.wait_ge(added[i], (B + 1) * (len(SETS[i]) - 1))
                add_weights(nc, acc[:, i % 2, :, :], psD, onesF).then_inc(total_used[i], 1)

            def body(gg, par, B, first=False, last=False):
                for u in range(JB):
                    if u < JB - 1:
                        scores(B, u + 1, par)
                    elif not last:
                        scores(B + 1, 0, par)
                    elif par == 0:
                        pe.wait_ge(q_loaded[1], gg * 80 + 80)
                        scores(B + 1, 0, 1)
                    if u == 0 and first:
                        pe.wait_ge(evacuated[1 - par], gg * 2 + 2 * par)
                        clear(psO, psD, zeros)
                    elif u == 0:
                        weights(B - 1, 2)
                    elif u == 4:
                        weights(B, 0)
                    elif u == 7:
                        weights(B, 1)
                    values(B, u)
                if last:
                    weights(B, 2)

            pe.wait_ge(zeros_set, 1)
            with pe.Fori(0, GG) as gg:
                for par in range(2):
                    B = (gg * 2 + par) * NB
                    if par == 0:
                        pe.wait_ge(q_loaded[0], gg * 80 + 80)
                        scores(B, 0, 0)
                    body(gg, par, B, first=True)
                    with pe.Fori(1, NB - 1) as q:
                        body(gg, par, B + q)
                    body(gg, par, B + (NB - 1), last=True)

        @block.scalar
        def _(act):
            def weights(B, u, par):
                wait_buffer(act, w_used, B, u)
                if u in (4, 5):
                    act.wait_ge(added[0], B * 2 + 1)
                elif u == 6:
                    act.wait_ge(added[0], B * 2 + 2)
                elif u == 7:
                    act.wait_ge(added[1], B * 2 + 1)
                elif u < 2:
                    act.wait_ge(added[1], B * 2)
                else:
                    act.wait_ge(added[2], B)
                for h in range(2):
                    act.wait_ge(scored[h][u // KB], B * KB + u % KB + 1)
                    nc.scalar.activation(w[:, u % NP, h, :], psS[h][:].rearrange("p a c -> p (a c)"), ACT.Exp,
                                         bias=shift_bc[:, par, h:h + 1], scale=SCALE).then_inc(exped[h], 1)

            def evacuate(gg, par):
                groups = gg * 2 + par + 1
                act.wait_ge(stored[par], gg * 48)
                act.wait_ge(w_used[JB - 1], groups * NB)
                nc.scalar.activation(o_sb[:, par, :], psO[:].rearrange("p a c -> p (a c)"), ACT.Copy
                                     ).then_inc(evacuated[par], 1)
                act.wait_ge(total_used[2], groups * NB)
                nc.scalar.activation(d_sb[:, par, :], psD[:], ACT.Copy).then_inc(evacuated[par], 1)

            with act.Fori(0, GG) as gg:
                B = gg * (2 * NB)
                act.wait_ge(q_loaded[0], gg * 80 + 80)
                with act.Fori(0, NB) as q:
                    for u in range(JB):
                        weights(B + q, u, 0)
                act.wait_ge(q_loaded[1], gg * 80 + 80)
                weights(B + NB, 0, 1)
                evacuate(gg, 0)
                for u in range(1, JB):
                    weights(B + NB, u, 1)
                with act.Fori(1, NB) as q:
                    for u in range(JB):
                        weights(B + NB + q, u, 1)
                evacuate(gg, 1)

        @block.vector
        def _(dve):
            with dve.Fori(0, CHUNKS) as ic:
                with dve.Fori(0, PAIRS) as pair:
                    with dve.Fori(0, NB) as q:
                        B = (ic * PAIRS + pair) * NB + q

                        def mask(u):
                            for h in range(2):
                                dve.wait_ge(exped[h], B * JB + u + 1)
                                nc.vector.tensor_tensor(w[:, u % NP, h, :], w[:, u % NP, h, :],
                                                        maskT[:, ds(q * JB + u, 1), ds(ic * IC, IC)]
                                                        .rearrange("p a c -> p (a c)"),
                                                        ALU.mult).then_inc(masked, 1)

                        def add(u, i):
                            k = SETS[i].index(u)
                            dve.wait_ge(masked, (B * JB + u) * 2 + 2)
                            if k == 1:
                                dve.wait_ge(total_used[2 - i], B + 1 if i == 2 else B)
                                other = w[:, (u - 1) % NP, :, :]
                            else:
                                dve.wait_ge(added[i], B * (len(SETS[i]) - 1) + k - 1)
                                other = acc[:, i % 2, :, :]
                            nc.vector.tensor_tensor(acc[:, i % 2, :, :], other, w[:, u % NP, :, :], ALU.add
                                                    ).then_inc(added[i], 1)

                        mask(0)
                        mask(1)
                        mask(2)
                        add(1, 0)
                        mask(3)
                        add(2, 0)
                        mask(4)
                        mask(5)
                        add(4, 1)
                        mask(6)
                        add(5, 1)
                        mask(7)
                        add(7, 2)

        @block.gpsimd
        def _(pool):
            pool.memset(zeros[:], 0.0).then_inc(zeros_set, 1)
            store_groups(pool, 1, 0, o_sb, d_sb, evacuated, stored, o_dram, d_dram)


_INS = ["x", "adj", "L0_gnn_W", "L0_gnn_b", "L0_gnn_att_l", "L0_gnn_att_r", "L1_gnn_x2", "L1_gnn_v"]


def kernel(**inputs):
    import numpy as _np
    import concourse.bacc as _bacc
    from concourse import mybir as _mybir
    from concourse.bass_utils import run_bass_kernel_spmd as _run

    nc = _bacc.Bacc("TRN2", target_bir_lowering=False, num_devices=1, dynamic_dma_scratch_size=4096)
    arrays, args = {}, []
    for name in _INS:
        a = _np.ascontiguousarray(inputs[name])
        arrays[f"in_{name}_dram"] = a
        args.append(nc.dram_tensor(f"in_{name}_dram", a.shape, _mybir.dt.from_np(a.dtype), kind="ExternalInput").ap())
    args.append(nc.dram_tensor("out_0_dram", (N, F), F32, kind="ExternalOutput").ap())
    gat_resnorm_kernel(nc, *args)
    r = _run(nc, [arrays], core_ids=[0])
    return r.results[0]["out_0_dram"]
```

```python
from contextlib import ExitStack

import concourse.bass as bass
from concourse import mybir

F32 = mybir.dt.float32
F16 = mybir.dt.float16
BF16 = mybir.dt.bfloat16
I32 = mybir.dt.int32
U8 = mybir.dt.uint8
ALU = mybir.AluOpType
ACT = mybir.ActivationFunctionType
AX = mybir.AxisListType
ds = bass.ds

P = 128
N = 4096
F = 512
H = 8
C = F // H
NT = N // P
PAIRS = H // 2
IC = 1024
HALF = 512
CHUNKS = N // IC
JB = 8
KB = 4
NB = NT // JB
NP = 4
SETS = ((0, 1, 2), (3, 4, 5, 6))
XW = 2 * C + 2
SCALE = float(C) ** -0.5
EPS = 1e-5
NO_EDGE = -9e15
LIMIT = 38.0


def gat_resnorm_kernel(nc, x, adj, W, b, att_l, att_r, x2, v, out):
    keep = ExitStack()
    with keep:
        def sb(name, shape, dt):
            return keep.enter_context(nc.sbuf_tensor(name, shape, dt))

        xl_dram = nc.dram_tensor("xl_scratch", [N, PAIRS, XW], F32).ap()
        al_dram = nc.dram_tensor("alpha_scratch", [2, H, N], F32).ap()
        k_dram = nc.dram_tensor("k_scratch", [2, F, N], F16).ap()
        q_dram = nc.dram_tensor("q_scratch", [2, F, N], F16).ap()
        shift_dram = nc.dram_tensor("shift_scratch", [2, H], F32).ap()
        o_dram = nc.dram_tensor("o_scratch", [2, PAIRS, P, N], F32).ap()
        d_dram = nc.dram_tensor("d_scratch", [2, H, N], F32).ap()
        x1_dram = nc.dram_tensor("x1_scratch", [N, F], F32).ap()

        maskT = sb("maskT", [P, NT, N], U8)
        identF = sb("identF", [P, P], F32)
        onesF = sb("onesF", [P, P], F32)
        headmask = sb("headmask", [H, F], BF16)
        colsum = sb("colsum", [H, F], F32)
        kmax = sb("kmax", [H, 1], F32)

        bounds = sb("bounds", [1, H], F32)
        least = sb("least", [1, 1], F32)
        wide = sb("wide", [1, 2], I32)

        prepare(nc, keep, x, adj, W, b, att_l, att_r, x2, xl_dram, al_dram, k_dram, shift_dram,
                maskT, identF, onesF, headmask, colsum, kmax, bounds, least, wide)
        sems = semaphores_of_either(nc, keep, 0)
        with nc.If(nc.values_load(wide[0:1, 0:1], min_val=0, max_val=1) > 0):
            attend_with_maximum(nc, sems(), 0, adj, xl_dram, al_dram, v, x1_dram, x2, o_dram, d_dram, identF)
        with nc.Else():
            attend_gat(nc, sems(), xl_dram, al_dram, shift_dram, o_dram, d_dram, maskT, onesF)
        finish_layer(nc, keep, 0, x, o_dram, d_dram, x1_dram, q_dram, shift_dram, v, identF, onesF, headmask,
                     colsum, kmax, bounds, least, wide)
        sems = semaphores_of_either(nc, keep, 1)
        with nc.If(nc.values_load(wide[0:1, 1:2], min_val=0, max_val=1) > 0):
            attend_with_maximum(nc, sems(), 1, adj, xl_dram, al_dram, v, x1_dram, x2, o_dram, d_dram, identF)
        with nc.Else():
            attend_dot(nc, sems(), v, q_dram, k_dram, shift_dram, o_dram, d_dram, maskT, onesF)
        finish_layer(nc, keep, 1, x1_dram, o_dram, d_dram, out, None, None, None, identF, onesF, headmask,
                     colsum, kmax, bounds, least, wide)


def semaphores_of_either(nc, keep, layer):
    taken = []

    def way():
        rest = list(taken)

        def sem(name):
            if rest:
                return rest.pop(0)
            taken.append(keep.enter_context(nc.semaphore(f"l{layer}_{name}")))
            return taken[-1]
        return sem
    return way


def prepare(nc, keep, x, adj, W, b, att_l, att_r, x2, xl_dram, al_dram, k_dram, shift_dram,
            maskT, identF, onesF, headmask, colsum, kmax, bounds, least, wide):
    ctx = ExitStack()
    with ctx:
        def sb(name, shape, dt):
            return ctx.enter_context(nc.sbuf_tensor(name, shape, dt))

        def ps(name, shape, dt):
            return ctx.enter_context(nc.psum_tensor(name, shape, dt))

        def sem(name):
            return keep.enter_context(nc.semaphore(name))

        QN = N // 4
        identB = sb("identB", [P, P], BF16)
        w_sb = sb("w_sb", [P, 5, F], F32)
        b_bc = w_sb[:, 4, :]
        att_bc = sb("att_bc", [P, 2, F], F32)
        wa_tmp = sb("wa_tmp", [P, 5, F], F32)
        wa = sb("wa", [P, 5, 40], F32)
        adj_sb = sb("adj_sb", [P, 4, QN], I32)
        mask_sb = sb("mask_sb", [P, 4, QN], BF16)
        x_sb = sb("x_sb", [P, 2, F], F32)
        x2_sb = sb("x2_sb", [P, 2, F], F32)
        xT = sb("xT", [P, 2, 4, P], F32)
        xl_sb = sb("xl_sb", [P, 2, PAIRS, XW], F32)
        kh = sb("kh", [P, PAIRS, KB * P], F16)
        kl = sb("kl", [P, PAIRS, KB * P], F16)
        sq = sb("sq", [P, F], F32)
        norms = sb("norms", [P, H], F32)
        norm_max = sb("norm_max", [P, H], F32)
        xl_sum = sb("xl_sum", [P, F], F32)
        alphaT = sb("alphaT", [40, KB * P], F32)
        ext_new = sb("ext_new", [40, 2], F32)
        ext = sb("ext", [40, 4], F32)
        ext_r = sb("ext_r", [H, 2], F32)
        shift = sb("shift", [H, 1], F32)

        psX = ps("psX", [P, 4, P], F32)
        psK = ps("psK", [P, 4, P], F32)
        psL = ps("psL", [P, F], F32)
        psA = ps("psA", [P, 512], F32)
        psM = [ps(f"psM{i}", [P, JB, P], BF16) for i in range(4)]
        alpha_nat = psA[:, 0:H]
        alpha_T = psA[0:40, P:2 * P]

        zeroed = sem("zeroed")
        consts = sem("consts")
        w_loaded = sem("w_loaded")
        dve_step = sem("dve_step")
        wa_ready = sem("wa_ready")
        adj_loaded = [sem(f"adj_loaded{i}") for i in range(4)]
        x_loaded = [sem(f"x_loaded{i}") for i in range(2)]
        x2_loaded = [sem(f"x2_loaded{i}") for i in range(2)]
        compared = [sem(f"compared{i}") for i in range(4)]
        turned = [sem(f"turned{i}") for i in range(4)]
        mask_out = [sem(f"mask_out{i}") for i in range(4)]
        x_turned = [sem(f"x_turned{i}") for i in range(2)]
        x2_turned = [sem(f"x2_turned{i}") for i in range(2)]
        xT_ready = [sem(f"xT_ready{i}") for i in range(2)]
        xl_ready = sem("xl_ready")
        alpha_ready = [sem(f"alpha_ready{i}") for i in range(2)]
        kh_ready = sem("kh_ready")
        kl_ready = sem("kl_ready")
        squared = [sem(f"squared{i}") for i in range(2)]
        reduced = sem("reduced")
        normed = sem("normed")
        xl_done = [sem(f"xl_done{i}") for i in range(2)]
        alpha_done = sem("alpha_done")
        summed = [sem(f"summed{i}") for i in range(2)]
        xl_stored = [sem(f"xl_stored{i}") for i in range(2)]
        k_stored = sem("k_stored")
        tail_pe = sem("tail_pe")
        tail_dve = sem("tail_dve")
        al_stored = sem("al_stored")
        ext_step = sem("ext_step")
        shift_stored = sem("shift_stored")

        block = ctx.enter_context(nc.Block())
        UN = KB
        R = NT // UN

        @block.sync
        def _(sp):
            sp.dma_start(w_sb[:, 0:4, :], W.rearrange("(k p) n -> p k n", p=P)).then_inc(w_loaded, 16)
            sp.dma_start(b_bc, b.partition_broadcast(P)).then_inc(w_loaded, 16)
            sp.dma_start(att_bc[:, 0, :], att_l.rearrange("h c -> (h c)").partition_broadcast(P)).then_inc(w_loaded, 16)
            sp.dma_start(att_bc[:, 1, :], att_r.rearrange("h c -> (h c)").partition_broadcast(P)).then_inc(w_loaded, 16)
            with sp.Fori(0, R) as r:
                for s in range(UN):
                    k, t, m = s % 2, r * UN + s, r * (UN // 2) + s // 2
                    rows = ds(t * P, P)
                    sp.wait_ge(x_turned[k], m)
                    sp.dma_start(x_sb[:, k, :], x[rows, :]).then_inc(x_loaded[k], 16)
                    sp.wait_ge(x2_turned[k], m)
                    sp.wait_ge(squared[k], m)
                    sp.dma_start(x2_sb[:, k, :], x2[rows, :]).then_inc(x2_loaded[k], 16)
                    for bank in range(4):
                        sp.wait_ge(compared[bank], t)
                        sp.dma_start(adj_sb[:, bank, :], adj[rows, bank * QN:(bank + 1) * QN]
                                     ).then_inc(adj_loaded[bank], 16)

        @block.gpsimd
        def _(pool):
            pool.memset(identF[:], 0.0).then_inc(zeroed, 1)
            pool.memset(identB[:], 0.0).then_inc(zeroed, 1)
            pool.memset(headmask[:], 1.0).then_inc(zeroed, 1)
            pool.memset(onesF[:], 1.0).then_inc(consts, 1)
            pool.wait_ge(zeroed, 3)
            for ident in (identF, identB):
                pool.affine_select(out=ident[:], in_=ident[:], compare_op=ALU.not_equal, fill=1.0, base=0,
                                   pattern=[[-1, P]], channel_multiplier=1).then_inc(consts, 1)
            pool.affine_select(out=headmask[:], in_=headmask[:], compare_op=ALU.is_ge, fill=0.0, base=0,
                               pattern=[[1, F]], channel_multiplier=-C).then_inc(zeroed, 1)
            pool.wait_ge(zeroed, 4)
            pool.affine_select(out=headmask[:], in_=headmask[:], compare_op=ALU.is_ge, fill=0.0, base=C - 1,
                               pattern=[[-1, F]], channel_multiplier=C).then_inc(consts, 1)
            pool.memset(xl_sum[:], 0.0).then_inc(consts, 1)
            pool.wait_ge(consts, 5)
            with pool.Fori(0, R) as r:
                for s in range(UN):
                    k, m = s % 2, r * (UN // 2) + s // 2
                    t = r * UN + s
                    pool.wait_ge(x2_loaded[k], m * 16 + 16)
                    pool.wait_ge(reduced, t)
                    pool.tensor_tensor(sq[:], x2_sb[:, k, :], x2_sb[:, k, :], ALU.mult).then_inc(squared[k], 1)
                    pool.wait_ge(xl_done[k], m * 2 + 2)
                    if k == 1:
                        pool.wait_ge(summed[0], m + 1)
                    else:
                        pool.wait_ge(summed[1], m)
                    pool.tensor_tensor(xl_sum[:].rearrange("p (a c) -> p a c", a=PAIRS),
                                       xl_sum[:].rearrange("p (a c) -> p a c", a=PAIRS),
                                       xl_sb[:, k, :, 0:2 * C], ALU.add).then_inc(summed[k], 1)
                    pool.dma_start(xl_dram[ds(t * P, P), :, :], xl_sb[:, k, :, :]).then_inc(xl_stored[k], 16)
            pool.wait_ge(tail_dve, 1)
            pool.dma_start(shift_dram[0].rearrange("(h o) -> h o", o=1), shift[:]).then_inc(shift_stored, 16)
            pool.wait_ge(shift_stored, 16)
            pool.dma_start(bounds[:], shift_dram[0:1, :]).then_inc(shift_stored, 16)
            for k in range(2):
                pool.wait_ge(xl_stored[k], 16 * (NT // 2))

        @block.scalar
        def _(act):
            with act.Fori(0, R) as r:
                for s in range(UN):
                    k, t, m = s % 2, r * UN + s, r * (UN // 2) + s // 2
                    act.wait_ge(x_turned[k], m + 1)
                    act.wait_ge(alpha_ready[k], m)
                    nc.scalar.activation(xT[:, k, :, :], psX[:], ACT.Copy).then_inc(xT_ready[k], 1)
                    act.wait_ge(x2_turned[k], m + 1)
                    if s == 0:
                        act.wait_ge(k_stored, r * 32)
                    nc.scalar.activation(kh[:, :, s * P:(s + 1) * P], psK[:], ACT.Copy).then_inc(kh_ready, 1)
                    for bank in range(4):
                        act.wait_ge(turned[bank], t + 1)
                        nc.scalar.activation(maskT[:, bank * JB:(bank + 1) * JB, ds(t * P, P)], psM[bank][:],
                                             ACT.Copy).then_inc(mask_out[bank], 1)
                act.wait_ge(kl_ready, r * UN + UN)
                for part, kk in enumerate((kh, kl)):
                    act.dma_start(k_dram[part].rearrange("(a p) n -> p a n", p=P)[:, :, ds(r * (KB * P), KB * P)],
                                   kk[:]).then_inc(k_stored, 16)
                act.wait_ge(alpha_done, r * UN + UN)
                for side in range(2):
                    act.dma_start(al_dram[side, :, ds(r * (KB * P), KB * P)], alphaT[32 * side:32 * side + H, :]
                                   ).then_inc(al_stored, 16)
            act.wait_ge(al_stored, 32 * R)
            act.wait_ge(k_stored, 32 * R)

        @block.tensor
        def _(pe):
            def turn_mask(t, bank):
                pe.wait_ge(compared[bank], t + 1)
                pe.wait_ge(mask_out[bank], t)
                for c in range(JB):
                    last = nc.tensor.transpose(psM[bank][:, c, :], mask_sb[:, bank, c * P:(c + 1) * P], identB[:])
                last.then_inc(turned[bank], 1)

            pe.wait_ge(consts, 5)
            with pe.Fori(0, R) as r:
                for s in range(UN):
                    k, t, m = s % 2, r * UN + s, r * (UN // 2) + s // 2
                    pe.wait_ge(x_loaded[k], m * 16 + 16)
                    if k == 1:
                        pe.wait_ge(xT_ready[0], m + 1)
                    else:
                        pe.wait_ge(xT_ready[1], m)
                    for c in range(4):
                        last = nc.tensor.transpose(psX[:, c, :], x_sb[:, k, c * P:(c + 1) * P], identF[:])
                    last.then_inc(x_turned[k], 1)
                    pe.wait_ge(x2_loaded[k], m * 16 + 16)
                    pe.wait_ge(kl_ready, t)
                    for c in range(4):
                        last = nc.tensor.transpose(psK[:, c, :], x2_sb[:, k, c * P:(c + 1) * P], identF[:])
                    last.then_inc(x2_turned[k], 1)
                    turn_mask(t, 0)
                    turn_mask(t, 1)
                    pe.wait_ge(xT_ready[k], m + 1)
                    if k == 1:
                        pe.wait_ge(xl_done[0], m * 2 + 2)
                    else:
                        pe.wait_ge(xl_done[1], m * 2)
                    for c in range(4):
                        last = nc.tensor.matmul(psL[:], xT[:, k, c, :], w_sb[:, c, :], start=(c == 0), stop=(c == 3))
                    last.then_inc(xl_ready, 1)
                    pe.wait_ge(wa_ready, 1)
                    pe.wait_ge(alpha_done, t)
                    for c in range(4):
                        nc.tensor.matmul(alpha_nat, xT[:, k, c, :], wa[:, c, 32:40], start=(c == 0), stop=False)
                    nc.tensor.matmul(alpha_nat, onesF[0:1, :], wa[0:1, 4, 32:40], start=False, stop=True)
                    for c in range(4):
                        nc.tensor.matmul(alpha_T, wa[:, c, :], xT[:, k, c, :], start=(c == 0), stop=False)
                    nc.tensor.matmul(alpha_T, wa[0:1, 4, :], onesF[0:1, :], start=False,
                                     stop=True).then_inc(alpha_ready[k], 1)
                    turn_mask(t, 2)
                    turn_mask(t, 3)
            for k in range(2):
                pe.wait_ge(summed[k], NT // 2)
            pe.wait_ge(kl_ready, NT)
            pe.wait_ge(xl_done[1], NT)
            nc.tensor.matmul(psL[0:H, :], onesF[:, 0:H], xl_sum[:], start=True, stop=True).then_inc(tail_pe, 1)
            pe.wait_ge(normed, NT)
            nc.tensor.transpose(psX[0:H, 0, :], norm_max[:], identF[:]).then_inc(tail_pe, 1)

        @block.vector
        def _(dve):
            steps = [0]

            def then(ins):
                steps[0] += 1
                ins.then_inc(dve_step, 1)
                dve.wait_ge(dve_step, steps[0])

            nc.vector.memset(wa[:], 0.0)
            nc.vector.memset(norm_max[:], 0.0)
            then(nc.vector.memset(ext[:], 0.0))
            dve.wait_ge(w_loaded, 64)
            for a in range(2):
                then(nc.vector.tensor_tensor(wa_tmp[:], w_sb[:], att_bc[:, a:a + 1, :].to_broadcast([P, 5, F]), ALU.mult))
                then(nc.vector.tensor_reduce(wa[:, :, 32 * a:32 * a + H],
                                             wa_tmp[:].rearrange("p k (h c) -> p k h c", h=H), AX.X, ALU.add))
            dve.sem_inc(wa_ready, 1)
            with dve.Fori(0, R) as r:
                for s in range(UN):
                    k, t, m = s % 2, r * UN + s, r * (UN // 2) + s // 2
                    for bank in range(4):
                        dve.wait_ge(adj_loaded[bank], t * 16 + 16)
                        dve.wait_ge(turned[bank], t)
                        nc.vector.tensor_scalar(mask_sb[:, bank, :], adj_sb[:, bank, :], 0.0, None,
                                                ALU.is_gt).then_inc(compared[bank], 1)
                    dve.wait_ge(kh_ready, t + 1)
                    nc.vector.tensor_tensor(kl[:, :, s * P:(s + 1) * P], psK[:], kh[:, :, s * P:(s + 1) * P],
                                            ALU.subtract).then_inc(kl_ready, 1)
                    dve.wait_ge(squared[k], m + 1)
                    dve.wait_ge(normed, t)
                    nc.vector.tensor_reduce(norms[:], sq[:].rearrange("p (h c) -> p h c", h=H), AX.X,
                                            ALU.add).then_inc(reduced, 1)
                    dve.wait_ge(xl_ready, t + 1)
                    dve.wait_ge(xl_stored[k], m * 16)
                    dve.wait_ge(summed[k], m)
                    nc.vector.tensor_tensor(xl_sb[:, k, :, 0:2 * C], psL[:].rearrange("p (a c) -> p a c", a=PAIRS),
                                            b_bc.rearrange("p (a c) -> p a c", a=PAIRS),
                                            ALU.add).then_inc(xl_done[k], 1)
                    dve.wait_ge(reduced, t + 1)
                    nc.vector.tensor_tensor(norm_max[:], norm_max[:], norms[:], ALU.max).then_inc(normed, 1)
                    dve.wait_ge(alpha_ready[k], m + 1)
                    nc.vector.tensor_copy(xl_sb[:, k, :, 2 * C:XW],
                                          alpha_nat.rearrange("p (a h) -> p a h", h=2)).then_inc(xl_done[k], 1)
                    if s == 0:
                        dve.wait_ge(al_stored, r * 32)
                    nc.vector.tensor_copy(alphaT[:, s * P:(s + 1) * P], alpha_T).then_inc(alpha_done, 1)
                dve.wait_ge(alpha_done, r * UN + UN)
                for i, op in enumerate((ALU.max, ALU.min)):
                    nc.vector.tensor_reduce(ext_new[:, i:i + 1], alphaT[:], AX.X, op).then_inc(ext_step, 1)
                dve.wait_ge(ext_step, r * 4 + 2)
                for i, op in enumerate((ALU.max, ALU.min)):
                    nc.vector.tensor_tensor(ext[:, i:i + 1], ext[:, i:i + 1], ext_new[:, i:i + 1], op).then_inc(ext_step, 1)
                dve.wait_ge(ext_step, r * 4 + 4)
            then(nc.vector.tensor_scalar(ext[:, 2:3], ext[:, 1:2], -1.0, None, ALU.mult))
            then(nc.vector.tensor_tensor(ext[:, 3:4], ext[:, 0:1], ext[:, 2:3], ALU.max))
            then(nc.vector.tensor_copy(ext_r[:, 0:1], ext[32:40, 3:4]))
            then(nc.vector.tensor_tensor(ext_r[:, 1:2], ext[0:H, 3:4], ext_r[:, 0:1], ALU.mult))
            nc.vector.tensor_scalar(shift[:], ext_r[:, 1:2], -1.0, None, ALU.mult).then_inc(tail_dve, 1)
            dve.wait_ge(tail_pe, 1)
            nc.vector.tensor_tensor(colsum[:], psL[0:H, :], headmask[:], ALU.mult)
            dve.wait_ge(tail_pe, 2)
            then(nc.vector.tensor_reduce(kmax[:], psX[0:H, 0, :], AX.X, ALU.max))
            dve.wait_ge(shift_stored, 32)
            then(nc.vector.tensor_reduce(least[:], bounds[:], AX.X, ALU.min))
            then(nc.vector.tensor_scalar(wide[:, 0:1], least[:], -LIMIT, None, ALU.is_lt))


def attend_gat(nc, sem, xl_dram, al_dram, shift_dram, o_dram, d_dram, maskT, onesF):
    clear = clear_with(nc)
    ctx = ExitStack()
    with ctx:
        def sb(name, shape, dt):
            return ctx.enter_context(nc.sbuf_tensor(name, shape, dt))

        def ps(name, shape, dt):
            return ctx.enter_context(nc.psum_tensor(name, shape, dt))

        al_bc = sb("al_bc", [P, 2, 2, IC], F32)
        shift_bc = sb("g_shift", [P, 2, 2], F32)
        xl = sb("g_xl", [P, 2, KB, XW], F32)
        w = sb("g_weights", [P, NP, 2, IC], F32)
        total = sb("g_total", [P, 2, IC], F32)
        o_sb = sb("g_o", [P, 2, IC], F32)
        d_sb = sb("g_d", [P, 2, HALF], F32)
        psO = [ps(f"g_psO{i}", [P, 2, HALF], F32) for i in range(2)]
        psD = [ps(f"g_psD{i}", [P, HALF], F32) for i in range(2)]
        zeros = sb("g_zeros", [1, HALF], BF16)
        zeros_set = sem("g_zeros_set")

        const_loaded = [sem(f"g_const_loaded{i}") for i in range(2)]
        const_used = [sem(f"g_const_used{i}") for i in range(2)]
        xl_loaded = [sem(f"g_xl_loaded{i}") for i in range(2)]
        exped = sem("g_exped")
        masked = sem("g_masked")
        w_used = [sem(f"g_w_used{u}") for u in range(JB)]
        added = sem("g_added")
        total_used = sem("g_total_used")
        cleared = sem("g_cleared")
        evacuated = [sem(f"g_evacuated{i}") for i in range(2)]
        stored = [sem(f"g_stored{i}") for i in range(2)]

        block = ctx.enter_context(nc.Block())

        @block.sync
        def _(sp):
            with sp.Fori(0, CHUNKS) as ic:
                with sp.Fori(0, PAIRS // 2) as pp:
                    for par in range(2):
                        pair, use = pp * 2 + par, ic * (PAIRS // 2) + pp
                        sp.wait_ge(const_used[par], use)
                        sp.dma_start(al_bc[:, par, :, :],
                                     al_dram[0, ds(pair * 2, 2), ds(ic * IC, IC)].partition_broadcast(P)
                                     ).then_inc(const_loaded[par], 16)
                        sp.dma_start(shift_bc[:, par, :],
                                     shift_dram[0, ds(pair * 2, 2)].partition_broadcast(P)
                                     ).then_inc(const_loaded[par], 16)
                        with sp.Fori(0, NB) as q:
                            for slot in range(2):
                                B = (use * 2 + par) * NB + q
                                sp.wait_ge(w_used[slot * KB + KB - 1], B)
                                sp.dma_start(xl[:, slot, :, :],
                                             xl_dram[ds(q * (JB * P) + slot * (KB * P), KB * P), ds(pair, 1), :]
                                             .rearrange("(t p) a c -> p (t a) c", p=P)).then_inc(xl_loaded[slot], 16)

        FIRST, SECOND = 2, 3
        GG = CHUNKS * PAIRS // 2

        @block.scalar
        def _(act):
            def weights(gg, par, B, u):
                slot = u // KB
                if u % KB == 0:
                    act.wait_ge(xl_loaded[slot], B * 16 + 16)
                wait_buffer(act, w_used, B, u)
                if u - NP in (FIRST, SECOND):
                    act.wait_ge(added, B + 1)
                for h in range(2):
                    nc.scalar.activation(w[:, u % NP, h, :], al_bc[:, par, h, :], ACT.Exp,
                                         bias=shift_bc[:, par, h:h + 1],
                                         scale=xl[:, slot, u % KB, 2 * C + h:2 * C + h + 1]).then_inc(exped, 1)

            def evacuate(groups, par):
                act.wait_ge(w_used[JB - 1], groups * NB)
                nc.scalar.activation(o_sb[:, par, :], psO[par][:].rearrange("p a c -> p (a c)"), ACT.Copy
                                     ).then_inc(evacuated[par], 1)
                nc.scalar.activation(d_sb[:, par, :], psD[par][:], ACT.Copy).then_inc(evacuated[par], 1)

            act.wait_ge(cleared, 1)
            with act.Fori(0, GG) as gg:
                for par in range(2):
                    G = gg * 2 + par
                    act.wait_ge(const_loaded[par], gg * 32 + 32)
                    for u in range(JB):
                        weights(gg, par, G * NB, u)
                        if u == 1:
                            evacuate(G, 1 - par)
                    with act.Fori(1, NB) as q:
                        for u in range(JB):
                            weights(gg, par, G * NB + q, u)
                    act.wait_ge(exped, (G + 1) * (2 * NT))
                    act.sem_inc(const_used[par], 1)
                    act.wait_ge(stored[par], gg * 48)
            evacuate(2 * GG, 1)

        @block.vector
        def _(dve):
            with dve.Fori(0, CHUNKS) as ic:
                with dve.Fori(0, PAIRS) as pair:
                    with dve.Fori(0, NB) as q:
                        B = (ic * PAIRS + pair) * NB + q
                        for u in range(JB):
                            for h in range(2):
                                dve.wait_ge(exped, (B * JB + u) * 2 + h + 1)
                                nc.vector.tensor_tensor(w[:, u % NP, h, :], w[:, u % NP, h, :],
                                                        maskT[:, ds(q * JB + u, 1), ds(ic * IC, IC)]
                                                        .rearrange("p a c -> p (a c)"),
                                                        ALU.mult).then_inc(masked, 1)
                            if u == SECOND + 1:
                                dve.wait_ge(total_used, B)
                                dve.wait_ge(masked, (B * JB + SECOND) * 2 + 2)
                                nc.vector.tensor_tensor(total[:], w[:, FIRST % NP, :, :], w[:, SECOND % NP, :, :],
                                                        ALU.add).then_inc(added, 1)

        @block.tensor
        def _(pe):
            pe.wait_ge(zeros_set, 1)
            clear(psO[1], psD[1], zeros).then_inc(cleared, 1)
            with pe.Fori(0, GG) as gg:
                for par in range(2):
                    pe.wait_ge(evacuated[par], gg * 2 + 2 * par)
                    clear(psO[par], psD[par], zeros)
                    with pe.Fori(0, NB) as q:
                        B = (gg * 2 + par) * NB + q
                        for u in range(JB):
                            n, slot = B * JB + u, u // KB
                            pe.wait_ge(xl_loaded[slot], B * 16 + 16)
                            pe.wait_ge(masked, n * 2 + 2)
                            last = add_values(nc, w[:, u % NP, :, :], xl[:, slot, u % KB, 0:2 * C], psO[par])
                            if u not in (FIRST, SECOND):
                                last = add_weights(nc, w[:, u % NP, :, :], psD[par], onesF)
                            last.then_inc(w_used[u], 1)
                            if u == SECOND + 1:
                                pe.wait_ge(added, B + 1)
                                add_weights(nc, total, psD[par], onesF).then_inc(total_used, 1)

        @block.gpsimd
        def _(pool):
            pool.memset(zeros[:], 0.0).then_inc(zeros_set, 1)
            store_groups(pool, 0, 1, o_sb, d_sb, evacuated, stored, o_dram, d_dram)


def clear_with(nc):
    def clear(psO, psD, zeros):
        for bank in (psO[:, 0, :], psO[:, 1, :], psD[:]):
            last = nc.tensor.matmul(bank, zeros[0:1, 0:P], zeros[0:1, :], start=True, stop=False, skip_group_check=True)
        return last
    return clear


def add_values(nc, w, values, psO):
    for hf in range(2):
        for h in range(2):
            last = nc.tensor.matmul(psO[h * C:(h + 1) * C, hf, :], values[:, h * C:(h + 1) * C],
                                    w[:, h, hf * HALF:(hf + 1) * HALF], start=False, stop=False, skip_group_check=True)
    return last


def add_weights(nc, w, psD, onesF):
    for hf in range(2):
        for h in range(2):
            row = 32 * (2 * h + hf)
            last = nc.tensor.matmul(psD[row:row + 32, :], onesF[:, 0:32], w[:, h, hf * HALF:(hf + 1) * HALF],
                                    start=False, stop=False, skip_group_check=True)
    return last


def wait_buffer(act, w_used, B, u):
    if u >= NP:
        act.wait_ge(w_used[u - NP], B + 1)
    else:
        act.wait_ge(w_used[u + JB - NP], B)


def store_groups(pool, layer, unstored, o_sb, d_sb, evacuated, stored, o_dram, d_dram):
    with pool.Fori(0, CHUNKS) as ic:
        with pool.Fori(0, PAIRS // 2) as pp:
            for par in range(2):
                pair, use = pp * 2 + par, ic * (PAIRS // 2) + pp
                pool.wait_ge(evacuated[par], use * 2 + 2 + 2 * unstored * par)
                pool.dma_start(o_dram[layer, ds(pair, 1), :, ds(ic * IC, IC)].rearrange("a p n -> (a p) n"),
                               o_sb[:, par, :]).then_inc(stored[par], 16)
                for hf in range(2):
                    pool.dma_start(d_dram[layer, ds(pair * 2, 2), ds(ic * IC + hf * HALF, HALF)],
                                   d_sb[32 * hf:P:64, par, :]).then_inc(stored[par], 16)
    for par in range(2):
        pool.wait_ge(stored[par], 48 * CHUNKS * PAIRS // 2)


def finish_layer(nc, keep, layer, x, o_dram, d_dram, result, q_dram, shift_dram, v, identF, onesF, headmask,
                 colsum, kmax, bounds, least, wide):
    first = layer == 0
    ctx = ExitStack()
    with ctx:
        def sb(name, shape, dt):
            return ctx.enter_context(nc.sbuf_tensor(f"f{layer}_{name}", shape, dt))

        def ps(name, shape, dt):
            return ctx.enter_context(nc.psum_tensor(f"f{layer}_{name}", shape, dt))

        def sem(name):
            return keep.enter_context(nc.semaphore(f"f{layer}_{name}"))

        T = 4
        R = NT // T
        oT = sb("oT", [P, 2, PAIRS, T * P], F32)
        xin = sb("xin", [P, 2, T, F], F32)
        dT = sb("dT", [H, 2, T * P], F32)
        alone = sb("alone", [H, 2, T * P], BF16)
        times_n = sb("times_n", [H, H], BF16)
        colparts = sb("colparts", [H, 3, F], BF16)
        rden = sb("rden", [P, T, H], F32)
        y = sb("y", [P, F], F32)
        z = sb("z", [P, T, F], F32)
        stats = sb("stats", [P, T, 6], F32)
        mv = sb("mv", [P, T, 2], F32)
        std = sb("std", [P, T], F32)
        rstd = sb("rstd", [P, T], F32)
        res = sb("res", [P, T, F], F32)
        eps = sb("eps", [P, 1], F32)
        psO = [ps(f"psO{i}", [P, F], F32) for i in range(2)]
        psR = [ps(f"psR{i}", [P, H], F32) for i in range(2)]

        consts_set = sem("consts_set")
        o_loaded = [sem(f"o_loaded{i}") for i in range(2)]
        x_loaded = [sem(f"x_loaded{i}") for i in range(2)]
        alone_set = sem("alone_set")
        turned = [sem(f"turned{i}") for i in range(2)]
        chain = sem("chain")
        added = [sem(f"added{i}") for i in range(2)]
        stats_seen = sem("stats_seen")
        var_ready = sem("var_ready")
        std_ready = sem("std_ready")
        rstd_ready = sem("rstd_ready")
        res_ready = sem("res_ready")
        res_stored = sem("res_stored")
        if first:
            qh = sb("qh", [P, PAIRS, T * P], F16)
            ql = sb("ql", [P, PAIRS, T * P], F16)
            sq = sb("sq", [P, T, F], F32)
            v_sb = sb("v", [P, T, F], F32)
            v_sum = sb("v_sum", [P, F], F32)
            norms = sb("norms", [P, T * H], F32)
            norm_max = sb("norm_max", [P, T * H], F32)
            norm_all = sb("norm_all", [P, H], F32)
            qmax = sb("qmax", [H, 4], F32)
            psQ = [ps(f"psQ{i}", [P, PAIRS, P], F32) for i in range(T)]
            q_turned = sem("q_turned")
            qh_ready = sem("qh_ready")
            ql_ready = sem("ql_ready")
            squared = sem("squared")
            reduced = sem("reduced")
            normed = sem("normed")
            v_cleared = sem("v_cleared")
            v_loaded = sem("v_loaded")
            v_summed = sem("v_summed")
            q_stored = sem("q_stored")
            tail = sem("tail")
            s_stored = sem("s_stored")

        block = ctx.enter_context(nc.Block())

        def for_bodies(engine, work):
            with engine.Fori(0, R // 2) as rr:
                for par in range(2):
                    work(rr * 2 + par, rr, par)

        def wait_last(engine, counts, rr, par):
            engine.wait_ge(counts[1 - par], (rr + par) * T)

        @block.sync
        def _(sp):
            def load(r, rr, par):
                rows = ds(r * (T * P), T * P)
                sp.wait_ge(turned[par], rr * T)
                sp.dma_start(dT[:, par, :], d_dram[layer, :, rows]).then_inc(o_loaded[par], 16)
                sp.dma_start(oT[:, par, :, :], o_dram[layer, :, :, rows].rearrange("a p n -> p a n")
                             ).then_inc(o_loaded[par], 16)
                sp.wait_ge(added[par], rr * T)
                sp.dma_start(xin[:, par, :, :], x[rows, :].rearrange("(t p) c -> p t c", p=P)).then_inc(x_loaded[par], 16)

            for_bodies(sp, load)

        @block.tensor
        def _(pe):
            def transposes(r, rr, par):
                pe.wait_ge(o_loaded[par], rr * 32 + 32)
                for s in range(T):
                    if s < 2:
                        wait_last(pe, added, rr, par)
                    else:
                        pe.wait_ge(added[par], rr * T + s - 1)
                    for a in range(PAIRS):
                        nc.tensor.matmul(psO[s % 2][:, a * P:(a + 1) * P], oT[:, par, a, s * P:(s + 1) * P], identF[:],
                                         start=(a == 0), stop=False, skip_group_check=True)
                    if s == 0:
                        pe.wait_ge(alone_set, r + 1)
                    for part in range(3):
                        nc.tensor.matmul(psO[s % 2][:], alone[:, par, s * P:(s + 1) * P], colparts[:, part, :], start=False,
                                         stop=(part == 2), skip_group_check=True)
                    nc.tensor.matmul(psR[s % 2][:], dT[:, par, s * P:(s + 1) * P], identF[0:H, 0:H],
                                     start=True, stop=False)
                    nc.tensor.matmul(psR[s % 2][:], alone[:, par, s * P:(s + 1) * P], times_n[:], start=False, stop=True
                                     ).then_inc(turned[par], 1)
                if first:
                    for s in range(T):
                        pe.wait_ge(res_ready, r * T + s + 1)
                        pe.wait_ge(ql_ready, r * T)
                        for a in range(PAIRS):
                            last = nc.tensor.transpose(psQ[s][:, a, :], res[:, s, a * P:(a + 1) * P], identF[:])
                        last.then_inc(q_turned, 1)

            pe.wait_ge(consts_set, 7)
            for_bodies(pe, transposes)
            if first:
                pe.wait_ge(tail, 1)
                for par in range(2):
                    pe.wait_ge(added[par], NT // 2)
                nc.tensor.transpose(psO[0][0:H, 0:P], norm_all[:], identF[:]).then_inc(tail, 1)
                pe.wait_ge(v_summed, NT)
                nc.tensor.matmul(psO[1][0:H, :], onesF[:, 0:H], v_sum[:], start=True, stop=True).then_inc(tail, 1)

        @block.scalar
        def _(act):
            def flag(rr, par):
                act.wait_ge(o_loaded[par], rr * 32 + 32)
                act.wait_ge(turned[par], rr * T)
                nc.scalar.activation(alone[:, par, :], dT[:, par, :], ACT.Relu, bias=1.0, scale=-1e34
                                     ).then_inc(alone_set, 1)

            def deviations(r, rr, par):
                if par == 0:
                    flag(rr, 0)
                act.wait_ge(var_ready, r * T + T)
                act.wait_ge(rstd_ready, r)
                nc.scalar.activation(std[:], mv[:, :, 1], ACT.Sqrt, bias=eps[:]).then_inc(std_ready, 1)
                if par == 0:
                    flag(rr, 1)
                if first:
                    for s in range(T):
                        act.wait_ge(q_turned, r * T + s + 1)
                        if s == 0:
                            act.wait_ge(q_stored, r * 32)
                        nc.scalar.activation(qh[:, :, s * P:(s + 1) * P], psQ[s][:], ACT.Copy).then_inc(qh_ready, 1)
                else:
                    act.wait_ge(res_ready, r * T + T)
                act.dma_start(result[ds(r * (T * P), T * P), :].rearrange("(t p) c -> p t c", p=P), res[:]
                              ).then_inc(res_stored, 16)

            act.wait_ge(consts_set, 2)
            for_bodies(act, deviations)
            if first:
                act.wait_ge(tail, 5)
                nc.scalar.activation(qmax[:, 2:3], qmax[:, 1:2], ACT.Sqrt).then_inc(tail, 1)
            act.wait_ge(res_stored, 16 * R)

        @block.gpsimd
        def _(pool):
            if first:
                pool.memset(v_sum[:], 0.0).then_inc(v_cleared, 1)
                pool.wait_ge(v_cleared, 1)
                with pool.Fori(0, R) as r:
                    pool.wait_ge(v_summed, r * T)
                    pool.dma_start(v_sb[:], v[ds(r * (T * P), T * P), :].rearrange("(t p) c -> p t c", p=P)
                                   ).then_inc(v_loaded, 16)
                    pool.wait_ge(v_loaded, r * 16 + 16)
                    for s in range(T):
                        pool.wait_ge(v_summed, r * T + s)
                        pool.tensor_tensor(v_sum[:], v_sum[:], v_sb[:, s, :], ALU.add).then_inc(v_summed, 1)
                    for s in range(T):
                        pool.wait_ge(res_ready, r * T + s + 1)
                        pool.wait_ge(reduced, r)
                        pool.tensor_tensor(sq[:, s, :], res[:, s, :], res[:, s, :], ALU.mult).then_inc(squared, 1)
                    pool.wait_ge(ql_ready, r * T + T)
                    for part, qq in enumerate((qh, ql)):
                        pool.dma_start(q_dram[part].rearrange("(a p) n -> p a n", p=P)[:, :, ds(r * (T * P), T * P)],
                                       qq[:]).then_inc(q_stored, 16)
                pool.wait_ge(tail, 7)
                pool.dma_start(shift_dram[1].rearrange("(h o) -> h o", o=1), qmax[:, 3:4]).then_inc(s_stored, 16)
                pool.wait_ge(s_stored, 16)
                pool.dma_start(bounds[:], shift_dram[1:2, :]).then_inc(s_stored, 16)
                pool.wait_ge(q_stored, 32 * R)

        @block.vector
        def _(dve):
            nc.vector.memset(eps[:], EPS).then_inc(consts_set, 1)
            if first:
                nc.vector.memset(norm_max[:], 0.0)
            nc.vector.tensor_scalar(times_n[:], identF[0:H, 0:H], float(N), None, ALU.mult).then_inc(consts_set, 1)
            whole = colsum[:]
            for part in range(3):
                nc.vector.tensor_copy(colparts[:, part, :], whole).then_inc(consts_set, 1)
                dve.wait_ge(consts_set, 3 + 2 * part)
                if part < 2:
                    nc.vector.tensor_tensor(y[0:H, :], whole, colparts[:, part, :], ALU.subtract
                                            ).then_inc(consts_set, 1)
                    dve.wait_ge(consts_set, 4 + 2 * part)
                    whole = y[0:H, :]
            LINKS = 3 * T

            def normalize(r, rr, par):
                for s in range(T):
                    dve.wait_ge(turned[par], rr * T + s + 1)
                    nc.vector.reciprocal(rden[:, s, :], psR[s % 2][:]).then_inc(chain, 1)
                    dve.wait_ge(chain, r * LINKS + 3 * s + 1)
                    nc.vector.tensor_tensor(y[:].rearrange("p (h c) -> p h c", h=H),
                                            psO[s % 2][:].rearrange("p (h c) -> p h c", h=H),
                                            rden[:, s, :].unsqueeze(2).to_broadcast([P, H, C]), ALU.mult
                                            ).then_inc(chain, 1)
                    if s == 0:
                        dve.wait_ge(x_loaded[par], rr * 16 + 16)
                    dve.wait_ge(chain, r * LINKS + 3 * s + 2)
                    if first:
                        ins = nc.vector.scalar_tensor_tensor(out=z[:, s, :], in0=y[:], scalar=0.0,
                                                             in1=xin[:, par, s, :], op0=ALU.max, op1=ALU.add)
                    else:
                        ins = nc.vector.tensor_tensor(z[:, s, :], y[:], xin[:, par, s, :], ALU.add)
                    ins.then_inc(added[par], 1)
                    dve.wait_ge(added[par], rr * T + s + 1)
                    nc.vector.bn_stats(stats[:, s, :], z[:, s, :]).then_inc(chain, 1)
                    dve.wait_ge(chain, r * LINKS + 3 * s + 3)
                    dve.sem_inc(stats_seen, 1)
                    nc.vector.bn_aggr(mv[:, s, :], stats[:, s, :]).then_inc(var_ready, 1)
                dve.wait_ge(std_ready, r + 1)
                nc.vector.reciprocal(rstd[:], std[:]).then_inc(rstd_ready, 1)
                dve.wait_ge(rstd_ready, r + 1)
                dve.wait_ge(res_stored, r * 16)
                for s in range(T):
                    nc.vector.tensor_scalar(res[:, s, :], z[:, s, :], mv[:, s, 0:1], rstd[:, s:s + 1],
                                            ALU.subtract, ALU.mult).then_inc(res_ready, 1)
                if first:
                    for s in range(T):
                        dve.wait_ge(qh_ready, r * T + s + 1)
                        nc.vector.tensor_tensor(ql[:, :, s * P:(s + 1) * P], psQ[s][:], qh[:, :, s * P:(s + 1) * P],
                                                ALU.subtract).then_inc(ql_ready, 1)
                    dve.wait_ge(squared, r * T + T)
                    nc.vector.tensor_reduce(norms[:], sq[:].rearrange("p t (h c) -> p (t h) c", h=H), AX.X, ALU.add
                                            ).then_inc(reduced, 1)
                    dve.wait_ge(reduced, r + 1)
                    nc.vector.tensor_tensor(norm_max[:], norm_max[:], norms[:], ALU.max).then_inc(normed, 1)

            for_bodies(dve, normalize)
            if first:
                dve.wait_ge(normed, R)
                nc.vector.tensor_reduce(norm_all[:], norm_max[:].rearrange("p (t h) -> p h t", h=H), AX.X, ALU.max
                                        ).then_inc(tail, 1)
                dve.wait_ge(tail, 3)
                nc.vector.tensor_tensor(colsum[:], psO[1][0:H, :], headmask[:], ALU.mult)
                nc.vector.tensor_reduce(qmax[:, 0:1], psO[0][0:H, 0:P], AX.X, ALU.max).then_inc(tail, 1)
                dve.wait_ge(tail, 4)
                nc.vector.tensor_tensor(qmax[:, 1:2], qmax[:, 0:1], kmax[:], ALU.mult).then_inc(tail, 1)
                dve.wait_ge(tail, 6)
                nc.vector.tensor_scalar(qmax[:, 3:4], qmax[:, 2:3], -SCALE, None, ALU.mult).then_inc(tail, 1)
                dve.wait_ge(s_stored, 32)
                nc.vector.tensor_reduce(least[:], bounds[:], AX.X, ALU.min).then_inc(tail, 1)
                dve.wait_ge(tail, 8)
                nc.vector.tensor_scalar(wide[:, 1:2], least[:], -LIMIT, None, ALU.is_lt).then_inc(tail, 1)


def attend_dot(nc, sem, v, q_dram, k_dram, shift_dram, o_dram, d_dram, maskT, onesF):
    clear = clear_with(nc)
    ctx = ExitStack()
    with ctx:
        def sb(name, shape, dt):
            return ctx.enter_context(nc.sbuf_tensor(f"a_{name}", shape, dt))

        def ps(name, shape, dt):
            return ctx.enter_context(nc.psum_tensor(f"a_{name}", shape, dt))

        q_sb = sb("q", [P, 2, 2, 2, IC], F16)
        shift_bc = sb("shift", [P, 2, 2], F32)
        k_sb = sb("k", [P, 2, 2, KB * P], F16)
        v_sb = sb("v", [P, 2, KB, 2 * C], F32)
        w = sb("weights", [P, NP, 2, IC], F32)
        total = sb("total", [P, 2, 2, IC], F32)
        o_sb = sb("o", [P, 2, IC], F32)
        d_sb = sb("d", [P, 2, HALF], F32)
        zeros = sb("zeros", [1, HALF], BF16)
        psS = [ps(f"psS{i}", [P, 2, HALF], F32) for i in range(2)]
        psO = ps("psO", [P, 2, HALF], F32)
        psD = ps("psD", [P, HALF], F32)

        zeros_set = sem("zeros_set")
        q_loaded = [sem(f"q_loaded{i}") for i in range(2)]
        k_loaded = [sem(f"k_loaded{i}") for i in range(2)]
        v_loaded = [sem(f"v_loaded{i}") for i in range(2)]
        scored = [[sem(f"scored{h}_{slot}") for slot in range(2)] for h in range(2)]
        exped = [sem(f"exped{i}") for i in range(2)]
        masked = sem("masked")
        w_used = [sem(f"w_used{u}") for u in range(JB)]
        added = {u: sem(f"added{u}") for s in SETS for u in s[1:]}
        total_used = [sem(f"total_used{i}") for i in range(2)]
        evacuated = [sem(f"evacuated{i}") for i in range(2)]
        stored = [sem(f"stored{i}") for i in range(2)]

        block = ctx.enter_context(nc.Block())
        GG = CHUNKS * PAIRS // 2

        @block.sync
        def _(sp):
            with sp.Fori(0, CHUNKS) as ic:
                with sp.Fori(0, PAIRS // 2) as pp:
                    for par in range(2):
                        pair, use = pp * 2 + par, ic * (PAIRS // 2) + pp
                        G = use * 2 + par
                        sp.wait_ge(evacuated[par], use * 2)
                        for twice in range(2):
                            for part in range(2):
                                sp.dma_start(q_sb[twice * C:(twice + 1) * C, par, part, :, :],
                                             q_dram[part, ds(pair * (2 * C), 2 * C), ds(ic * IC, IC)]
                                             .rearrange("(h c) n -> c h n", h=2)).then_inc(q_loaded[par], 16)
                        sp.dma_start(shift_bc[:, par, :], shift_dram[1, ds(pair * 2, 2)].partition_broadcast(P)
                                     ).then_inc(q_loaded[par], 16)
                        with sp.Fori(0, NB) as q:
                            for slot in range(2):
                                B = G * NB + q
                                src = q * (JB * P) + slot * (KB * P)
                                sp.wait_ge(scored[1][slot], B * KB)
                                for part in range(2):
                                    sp.dma_start(k_sb[part * C:(part + 1) * C, slot, :, :],
                                                 k_dram[part, ds(pair * (2 * C), 2 * C), ds(src, KB * P)]
                                                 .rearrange("(h c) n -> c h n", h=2)).then_inc(k_loaded[slot], 16)
                                sp.wait_ge(w_used[slot * KB + KB - 1], B)
                                sp.dma_start(v_sb[:, slot, :, :],
                                             v[ds(src, KB * P), ds(pair * (2 * C), 2 * C)]
                                             .rearrange("(t p) c -> p t c", p=P)).then_inc(v_loaded[slot], 16)

        @block.tensor
        def _(pe):
            def scores(B, u, par):
                n, slot = B * JB + u, u // KB
                if u % KB == 0:
                    pe.wait_ge(k_loaded[slot], B * 32 + 32)
                for h in range(2):
                    pe.wait_ge(exped[h], n)
                    for hf in range(2):
                        for part in range(2):
                            last = nc.tensor.matmul(psS[h][:, hf, :],
                                                    k_sb[:, slot, h, (u % KB) * P:(u % KB + 1) * P],
                                                    q_sb[:, par, part, h, hf * HALF:(hf + 1) * HALF],
                                                    start=(part == 0), stop=(part == 1))
                    last.then_inc(scored[h][slot], 1)

            def values(B, u):
                n, slot = B * JB + u, u // KB
                if u % KB == 0:
                    pe.wait_ge(v_loaded[slot], B * 16 + 16)
                pe.wait_ge(masked, n * 2 + 2)
                last = add_values(nc, w[:, u % NP, :, :], v_sb[:, slot, u % KB, :], psO)
                if u == JB - 1:
                    last = add_weights(nc, w[:, u % NP, :, :], psD, onesF)
                last.then_inc(w_used[u], 1)

            def weights(B, i):
                pe.wait_ge(added[SETS[i][-1]], B * 2 + 2)
                add_weights(nc, total[:, i, :, :], psD, onesF).then_inc(total_used[i], 1)

            def body(gg, par, B, first=False, last=False):
                for u in range(JB):
                    if u < JB - 1:
                        scores(B, u + 1, par)
                    elif not last:
                        scores(B + 1, 0, par)
                    elif par == 0:
                        pe.wait_ge(q_loaded[1], gg * 80 + 80)
                        scores(B + 1, 0, 1)
                    if u == 0 and first:
                        pe.wait_ge(evacuated[1 - par], gg * 2 + 2 * par)
                        clear(psO, psD, zeros)
                    elif u == 0:
                        weights(B - 1, 1)
                    elif u == 5:
                        weights(B, 0)
                    values(B, u)
                if last:
                    weights(B, 1)

            pe.wait_ge(zeros_set, 1)
            with pe.Fori(0, GG) as gg:
                for par in range(2):
                    B = (gg * 2 + par) * NB
                    if par == 0:
                        pe.wait_ge(q_loaded[0], gg * 80 + 80)
                        scores(B, 0, 0)
                    body(gg, par, B, first=True)
                    with pe.Fori(1, NB - 1) as q:
                        body(gg, par, B + q)
                    body(gg, par, B + (NB - 1), last=True)

        @block.scalar
        def _(act):
            def weights(B, u, par):
                wait_buffer(act, w_used, B, u)
                if u >= NP:
                    act.wait_ge(added[u - NP if u - NP in added else u - NP + 1], B * 2 + 2)
                elif u + NP in added:
                    act.wait_ge(added[u + NP], B * 2)
                for h in range(2):
                    act.wait_ge(scored[h][u // KB], B * KB + u % KB + 1)
                    nc.scalar.activation(w[:, u % NP, h, :], psS[h][:].rearrange("p a c -> p (a c)"), ACT.Exp,
                                         bias=shift_bc[:, par, h:h + 1], scale=SCALE).then_inc(exped[h], 1)

            def evacuate(gg, par):
                groups = gg * 2 + par + 1
                act.wait_ge(stored[par], gg * 48)
                act.wait_ge(w_used[JB - 1], groups * NB)
                nc.scalar.activation(o_sb[:, par, :], psO[:].rearrange("p a c -> p (a c)"), ACT.Copy
                                     ).then_inc(evacuated[par], 1)
                act.wait_ge(total_used[1], groups * NB)
                nc.scalar.activation(d_sb[:, par, :], psD[:], ACT.Copy).then_inc(evacuated[par], 1)

            with act.Fori(0, GG) as gg:
                B = gg * (2 * NB)
                act.wait_ge(q_loaded[0], gg * 80 + 80)
                with act.Fori(0, NB) as q:
                    for u in range(JB):
                        weights(B + q, u, 0)
                act.wait_ge(q_loaded[1], gg * 80 + 80)
                weights(B + NB, 0, 1)
                evacuate(gg, 0)
                for u in range(1, JB):
                    weights(B + NB, u, 1)
                with act.Fori(1, NB) as q:
                    for u in range(JB):
                        weights(B + NB + q, u, 1)
                evacuate(gg, 1)

        @block.vector
        def _(dve):
            with dve.Fori(0, CHUNKS) as ic:
                with dve.Fori(0, PAIRS) as pair:
                    with dve.Fori(0, NB) as q:
                        B = (ic * PAIRS + pair) * NB + q

                        def mask(u):
                            for h in range(2):
                                dve.wait_ge(exped[h], B * JB + u + 1)
                                nc.vector.tensor_tensor(w[:, u % NP, h, :], w[:, u % NP, h, :],
                                                        maskT[:, ds(q * JB + u, 1), ds(ic * IC, IC)]
                                                        .rearrange("p a c -> p (a c)"),
                                                        ALU.mult).then_inc(masked, 1)

                        def add(u, h):
                            i = 0 if u in SETS[0] else 1
                            dve.wait_ge(masked, (B * JB + u) * 2 + 1 + h)
                            if u == SETS[i][1]:
                                dve.wait_ge(total_used[i], B)
                                other = w[:, (u - 1) % NP, h, :]
                            else:
                                dve.wait_ge(added[u - 1], B * 2 + 1 + h)
                                other = total[:, i, h, :]
                            nc.vector.tensor_tensor(total[:, i, h, :], other, w[:, u % NP, h, :], ALU.add
                                                    ).then_inc(added[u], 1)

                        for u, additions in enumerate(((), ((1, 0), (1, 1)), ((2, 0),), ((2, 1),), ((4, 0), (4, 1)),
                                                       ((5, 0),), ((5, 1),), ((6, 0), (6, 1)))):
                            mask(u)
                            for tile, h in additions:
                                add(tile, h)

        @block.gpsimd
        def _(pool):
            pool.memset(zeros[:], 0.0).then_inc(zeros_set, 1)
            store_groups(pool, 1, 0, o_sb, d_sb, evacuated, stored, o_dram, d_dram)


def attend_with_maximum(nc, sem, layer, adj, xl_dram, al_dram, v, x1_dram, x2, o_dram, d_dram, identF):
    ctx = ExitStack()
    with ctx:
        def sb(name, shape, dt):
            return ctx.enter_context(nc.sbuf_tensor(f"m{layer}_{name}", shape, dt))

        def ps(name, shape, dt):
            return ctx.enter_context(nc.psum_tensor(f"m{layer}_{name}", shape, dt))

        scale = (1.0, SCALE)[layer]
        ROUND = 4
        s = sb("s", [P, N], F32)
        adj_sb = sb("adj", [P, N], I32)
        wT = sb("wT", [P, NT, P], F32)
        values = sb("values", [P, NT, C], F32)
        row_max = sb("row_max", [P, 1], F32)
        minus_max = sb("minus_max", [P, 1], F32)
        row_sum = sb("row_sum", [P, 1], F32)
        o_sb = sb("o", [C, P], F32)
        if layer == 0:
            ar_bc = sb("ar_bc", [P, N], F32)
            al = sb("al", [P, 1], F32)
        else:
            kT = sb("kT", [C, N], F32)
            q_sb = sb("q", [P, C], F32)
            qT = sb("qT", [C, P], F32)
            psS = ps("psS", [P, 4, HALF], F32)
        psT = [ps(f"psT{i}", [P, ROUND, P], F32) for i in range(2)]
        psO = ps("psO", [C, P], F32)

        head_loaded = sem("head_loaded")
        rows_loaded = sem("rows_loaded")
        scored = sem("scored")
        copied = sem("copied")
        step = sem("step")
        bounded = sem("bounded")
        exped = sem("exped")
        turned = sem("turned")
        taken = sem("taken")
        key_turned = sem("key_turned")
        key_taken = sem("key_taken")
        q_turned = sem("q_turned")
        q_taken = sem("q_taken")
        summed = sem("summed")
        ready = sem("ready")
        stored = sem("stored")
        HEAD = ROWS = 32
        ROUNDS = NT // ROUND

        block = ctx.enter_context(nc.Block())

        def for_tiles(engine, work, new_head=None):
            with engine.Fori(0, PAIRS) as pair:
                for hh in range(2):
                    g = pair * 2 + hh
                    if new_head:
                        new_head(g, pair, hh)
                    with engine.Fori(0, NT) as it:
                        work(g, g * NT + it, pair, hh, it)

        @block.sync
        def _(sp):
            def load_head(g, pair, hh):
                sp.wait_ge(stored, g * (32 * NT))
                if layer == 0:
                    sp.dma_start(ar_bc[:], al_dram[1, ds(pair * 2 + hh, 1), :].partition_broadcast(P)
                                 .rearrange("p a n -> p (a n)")).then_inc(head_loaded, 16)
                    sp.dma_start(values[:], xl_dram[:, ds(pair, 1), hh * C:(hh + 1) * C]
                                 .rearrange("(t p) a c -> p (t a) c", p=P)).then_inc(head_loaded, 16)
                else:
                    sp.dma_start(wT[:, :, 0:C], x2[:, ds(g * C, C)].rearrange("(t p) c -> p t c", p=P)
                                 ).then_inc(head_loaded, 16)
                    sp.dma_start(values[:], v[:, ds(g * C, C)].rearrange("(t p) c -> p t c", p=P)).then_inc(head_loaded, 16)

            def rows(g, n, pair, hh, it):
                sp.wait_ge(stored, n * 32)
                sp.dma_start(adj_sb[:], adj[ds(it * P, P), :]).then_inc(rows_loaded, 16)
                if layer == 0:
                    sp.dma_start(al[:], al_dram[0, ds(g, 1), ds(it * P, P)].rearrange("a p -> p a")
                                 ).then_inc(rows_loaded, 16)
                else:
                    sp.dma_start(q_sb[:], x1_dram[ds(it * P, P), ds(g * C, C)]).then_inc(rows_loaded, 16)
                sp.wait_ge(ready, n * 2 + 2)
                sp.dma_start(o_dram[layer, ds(pair, 1), hh * C:(hh + 1) * C, ds(it * P, P)]
                             .rearrange("a c n -> (a c) n"), o_sb[:]).then_inc(stored, 16)
                sp.dma_start(d_dram[layer, ds(g, 1), ds(it * P, P)].rearrange("a p -> p a"), row_sum[:]
                             ).then_inc(stored, 16)

            for_tiles(sp, rows, load_head)
            sp.wait_ge(stored, 32 * H * NT)

        @block.tensor
        def _(pe):
            def turn_keys(g, pair, hh):
                pe.wait_ge(head_loaded, g * HEAD + HEAD)
                pe.wait_ge(summed, g * NT)
                for k in range(ROUNDS):
                    pe.wait_ge(key_taken, g * ROUNDS + max(k - 1, 0))
                    for c in range(ROUND):
                        last = nc.tensor.matmul(psT[k % 2][0:C, c, :], wT[:, k * ROUND + c, 0:C], identF[:],
                                                start=True, stop=True)
                    last.then_inc(key_turned, 1)

            def rows(g, n, pair, hh, it):
                pe.wait_ge(head_loaded, g * HEAD + HEAD)
                pe.wait_ge(rows_loaded, n * ROWS + ROWS)
                if layer == 1:
                    pe.wait_ge(key_taken, g * ROUNDS + ROUNDS)
                    nc.tensor.matmul(psT[0][0:C, 0, :], q_sb[:], identF[:], start=True, stop=True).then_inc(q_turned, 1)
                    pe.wait_ge(q_taken, n + 1)
                if layer == 1:
                    for half in range(2):
                        pe.wait_ge(copied, n * 2 + half)
                        for bank in range(4):
                            last = nc.tensor.matmul(psS[:, bank, :], qT[:],
                                                    kT[:, (half * 4 + bank) * HALF:(half * 4 + bank + 1) * HALF],
                                                    start=True, stop=True)
                        last.then_inc(scored, 1)
                pe.wait_ge(exped, n + 1)
                for k in range(ROUNDS):
                    pe.wait_ge(taken, n * ROUNDS + max(k - 1, 0))
                    for c in range(ROUND):
                        last = nc.tensor.transpose(psT[k % 2][:, c, :], s[:, (k * ROUND + c) * P:(k * ROUND + c + 1) * P],
                                                   identF[:])
                    last.then_inc(turned, 1)
                pe.wait_ge(taken, n * ROUNDS + ROUNDS)
                for j in range(NT):
                    last = nc.tensor.matmul(psO[:], values[:, j, :], wT[:, j, :], start=(j == 0), stop=(j == NT - 1))
                last.then_inc(summed, 1)

            for_tiles(pe, rows, turn_keys if layer == 1 else None)

        @block.scalar
        def _(act):
            def take_keys(g, pair, hh):
                for k in range(ROUNDS):
                    act.wait_ge(key_turned, g * ROUNDS + k + 1)
                    nc.scalar.activation(kT[:, k * ROUND * P:(k + 1) * ROUND * P],
                                         psT[k % 2][0:C, :, :].rearrange("p a c -> p (a c)"), ACT.Copy).then_inc(key_taken, 1)

            def rows(g, n, pair, hh, it):
                if layer == 1:
                    act.wait_ge(q_turned, n + 1)
                    nc.scalar.activation(qT[:], psT[0][0:C, 0, :], ACT.Copy).then_inc(q_taken, 1)
                    for half in range(2):
                        act.wait_ge(scored, n * 2 + half + 1)
                        nc.scalar.activation(s[:, half * (N // 2):(half + 1) * (N // 2)],
                                             psS[:].rearrange("p a c -> p (a c)"), ACT.Copy).then_inc(copied, 1)
                act.wait_ge(bounded, n + 1)
                nc.scalar.activation(s[:], s[:], ACT.Exp, bias=minus_max[:], scale=scale).then_inc(exped, 1)
                for k in range(ROUNDS):
                    act.wait_ge(turned, n * ROUNDS + k + 1)
                    nc.scalar.activation(wT[:, k * ROUND:(k + 1) * ROUND, :], psT[k % 2][:], ACT.Copy).then_inc(taken, 1)
                act.wait_ge(summed, n + 1)
                nc.scalar.activation(o_sb[:], psO[:], ACT.Copy).then_inc(ready, 1)

            for_tiles(act, rows, take_keys if layer == 1 else None)

        @block.vector
        def _(dve):
            def rows(g, n, pair, hh, it):
                STEPS = (5, 4)[layer]
                steps = [0]

                def then(ins):
                    steps[0] += 1
                    ins.then_inc(step, 1)
                    dve.wait_ge(step, n * STEPS + steps[0])

                fill = wT[:].rearrange("p t i -> p (t i)")
                dve.wait_ge(rows_loaded, n * ROWS + ROWS)
                if layer == 0:
                    dve.wait_ge(head_loaded, g * HEAD + HEAD)
                    then(nc.vector.tensor_scalar(s[:], ar_bc[:], al[:], None, ALU.mult))
                else:
                    dve.wait_ge(copied, n * 2 + 2)
                then(nc.vector.tensor_scalar(fill, adj_sb[:], 0.0, NO_EDGE / scale, ALU.is_le, ALU.mult))
                then(nc.vector.scalar_tensor_tensor(out=s[:], in0=adj_sb[:], scalar=0.0, in1=s[:],
                                                    op0=ALU.is_gt, op1=ALU.mult))
                then(nc.vector.tensor_tensor(s[:], s[:], fill, ALU.add))
                then(nc.vector.tensor_reduce(row_max[:], s[:], AX.X, ALU.max))
                nc.vector.tensor_scalar(minus_max[:], row_max[:], -scale, None, ALU.mult).then_inc(bounded, 1)
                dve.wait_ge(exped, n + 1)
                nc.vector.tensor_reduce(row_sum[:], s[:], AX.X, ALU.add).then_inc(ready, 1)

            for_tiles(dve, rows)


_INS = ["x", "adj", "L0_gnn_W", "L0_gnn_b", "L0_gnn_att_l", "L0_gnn_att_r", "L1_gnn_x2", "L1_gnn_v"]


def kernel(**inputs):
    import numpy as _np
    import concourse.bacc as _bacc
    from concourse import mybir as _mybir
    from concourse.bass_utils import run_bass_kernel_spmd as _run

    nc = _bacc.Bacc("TRN2", target_bir_lowering=False, num_devices=1, dynamic_dma_scratch_size=4096)
    arrays, args = {}, []
    for name in _INS:
        a = _np.ascontiguousarray(inputs[name])
        arrays[f"in_{name}_dram"] = a
        args.append(nc.dram_tensor(f"in_{name}_dram", a.shape, _mybir.dt.from_np(a.dtype), kind="ExternalInput").ap())
    args.append(nc.dram_tensor("out_0_dram", (N, F), F32, kind="ExternalOutput").ap())
    gat_resnorm_kernel(nc, *args)
    r = _run(nc, [arrays], core_ids=[0])
    return r.results[0]["out_0_dram"]
```
